# Optimizing a Trainium2 kernel written in Bass

```python
import numpy as np
import jax
import jax.numpy as jnp

def _softmax(x, axis=-1):
    return jax.nn.softmax(x, axis=axis)
def _gelu(x):
    return jax.nn.gelu(x, approximate=True)
def _silu(x):
    return jax.nn.silu(x)
def _sigmoid(x):
    return jax.nn.sigmoid(x)
def _layernorm(x, axis=-1, eps=1e-5):
    m = jnp.mean(x, axis=axis, keepdims=True)
    v = jnp.var(x, axis=axis, keepdims=True)
    return (x - m) / jnp.sqrt(v + eps)
def _scatter_add(tgt, idx, src, axis=0):
    return tgt.at[idx].add(src)
def _segment_sum(src, seg, n):
    return jax.ops.segment_sum(src, seg, n)

kernel_name = 'mk_adj_resnorm_d2_adj_512_d5411a'

def setup_inputs(seed: int = 0):
    np.random.seed(seed)
    _w = jnp.asarray
    def _rec_inputs():
        import jax
        import jax.numpy as jnp
        _gk = jax.random.key(seed)
        x = -0.0002928 + 1 * jax.random.normal(jax.random.fold_in(_gk, 1), (4096, 512), jnp.float32)
        _a = jax.random.bernoulli(jax.random.fold_in(_gk, 2), 0.00390625, (4096, 4096))
        _a = jnp.logical_or(_a, jnp.swapaxes(_a, -1, -2))
        _a = jnp.logical_or(_a, jnp.eye(4096, dtype=bool))
        _af = _a.astype(jnp.float32)
        _af = _af * jax.random.uniform(jax.random.fold_in(_gk, 3), (4096, 4096), jnp.float32, 0.05, 5.41998)
        adj = _af
        return x, adj
    x, adj = _rec_inputs()
    def _L0_gnn_setup():
        import jax, jax.numpy as jnp
        import numpy as np
        N = 8192
        D = 512
        key = jax.random.key(seed)
        ks = jax.random.split(key, 6)
        s = 1.0 / np.sqrt(D)
        return {'x': jax.random.normal(ks[0], (N, D), jnp.float32), 'spatial_encoding': jax.random.normal(ks[1], (N, N), jnp.float32), 'edge_encoding': jax.random.normal(ks[2], (N, N), jnp.float32), 'Wq': jax.random.normal(ks[3], (D, D), jnp.float32) * s, 'bq': jnp.zeros((D,), jnp.float32), 'Wk': jax.random.normal(ks[4], (D, D), jnp.float32) * s, 'bk': jnp.zeros((D,), jnp.float32), 'Wv': jax.random.normal(ks[5], (D, D), jnp.float32) * s, 'bv': jnp.zeros((D,), jnp.float32)}
    _L0_gnn_all = _L0_gnn_setup()
    _L0_gnn_in = {k: v for k, v in _L0_gnn_all.items() if k in ('Wq', 'bq', 'Wk', 'bk', 'Wv', 'bv', )}
    del _L0_gnn_all

    def _L1_gnn_setup():
        import jax, jax.numpy as jnp
        import numpy as np
        N, NFEAT, NHID = (10000, 512, 128)
        key = jax.random.key(seed)
        k_x, k_adj, k_w1, k_b1, k_w2, k_b2 = jax.random.split(key, 6)
        x = jax.random.normal(k_x, (N, NFEAT), dtype=jnp.float32)
        adj = jax.random.uniform(k_adj, (N, N), dtype=jnp.float32)
        s1 = 1.0 / np.sqrt(NHID)
        s2 = 1.0 / np.sqrt(NFEAT)
        W1 = jax.random.uniform(k_w1, (NFEAT, NHID), minval=-s1, maxval=s1, dtype=jnp.float32)
        b1 = jax.random.uniform(k_b1, (NHID,), minval=-s1, maxval=s1, dtype=jnp.float32)
        W2 = jax.random.uniform(k_w2, (NHID, NFEAT), minval=-s2, maxval=s2, dtype=jnp.float32)
        b2 = jax.random.uniform(k_b2, (NFEAT,), minval=-s2, maxval=s2, dtype=jnp.float32)
        return {'x': x, 'adj': adj, 'W1': W1, 'b1': b1, 'W2': W2, 'b2': b2}
    _L1_gnn_all = _L1_gnn_setup()
    _L1_gnn_in = {k: v for k, v in _L1_gnn_all.items() if k in ('W1', 'b1', 'W2', 'b2', )}
    del _L1_gnn_all

    return {
        "x": x,
        "adj": adj,
        "L0_gnn_Wq": _L0_gnn_in["Wq"],
        "L0_gnn_bq": _L0_gnn_in["bq"],
        "L0_gnn_Wk": _L0_gnn_in["Wk"],
        "L0_gnn_bk": _L0_gnn_in["bk"],
        "L0_gnn_Wv": _L0_gnn_in["Wv"],
        "L0_gnn_bv": _L0_gnn_in["bv"],
        "L1_gnn_W1": _L1_gnn_in["W1"],
        "L1_gnn_b1": _L1_gnn_in["b1"],
        "L1_gnn_W2": _L1_gnn_in["W2"],
        "L1_gnn_b2": _L1_gnn_in["b2"],
    }

def reference(x, adj, L0_gnn_Wq, L0_gnn_bq, L0_gnn_Wk, L0_gnn_bk, L0_gnn_Wv, L0_gnn_bv, L1_gnn_W1, L1_gnn_b1, L1_gnn_W2, L1_gnn_b2):
    import jax
    import jax.numpy as jnp
    def _L0_gnn_ref(x, spatial_encoding, edge_encoding, Wq, bq, Wk, bk, Wv, bv):
        import jax, jax.numpy as jnp
        import numpy as np
        N = 8192
        D = 512
        q = x @ Wq.T + bq
        k = x @ Wk.T + bk
        v = x @ Wv.T + bv
        scale = 1.0 / jnp.sqrt(jnp.asarray(q.shape[-1], q.dtype))
        a = q @ k.T * scale + spatial_encoding + edge_encoding
        attn = jax.nn.softmax(a, axis=-1)
        return attn @ v

    def _L1_gnn_ref(x, adj, W1, b1, W2, b2):
        import jax, jax.numpy as jnp
        import numpy as np
        N, NFEAT, NHID = (10000, 512, 128)
        h = jax.nn.relu(adj @ (x @ W1) + b1)
        out = adj @ (h @ W2) + b2
        return out

    x = _layernorm(x + _L0_gnn_ref(x, adj, adj, L0_gnn_Wq, L0_gnn_bq, L0_gnn_Wk, L0_gnn_bk, L0_gnn_Wv, L0_gnn_bv), axis=-1)
    x = _layernorm(x + _L1_gnn_ref(x, adj, L1_gnn_W1, L1_gnn_b1, L1_gnn_W2, L1_gnn_b2), axis=-1)
    return x


_drawn_inputs = setup_inputs


def setup_inputs(seed=0):
    import zlib

    import numpy as np

    out = dict(_drawn_inputs(seed))
    spreads = {'L0_gnn_bq': (0.0, 0.396), 'L0_gnn_bk': (0.0, 2.0), 'L0_gnn_bv': (0.0, 0.1)}
    factors = {'L1_gnn_b1': 23.096, 'L1_gnn_b2': 64.0}
    for name, (base, spread) in spreads.items():
        noise = np.random.default_rng([zlib.crc32(name.encode()), seed]).standard_normal(out[name].shape)
        drawn = base * np.exp(spread * noise) if base else spread * noise
        out[name] = jnp.asarray(drawn.astype(out[name].dtype))
    for name, factor in factors.items():
        out[name] = (out[name] * factor).astype(out[name].dtype)
    return out
```

```python
import math
from contextlib import ExitStack

import concourse.bass as bass
from concourse import mybir

F32 = mybir.dt.float32
F16 = mybir.dt.float16
BF16 = mybir.dt.bfloat16
U32 = mybir.dt.uint32
ALU = mybir.AluOpType
ACT = mybir.ActivationFunctionType
AX = mybir.AxisListType.X
ALL_MAX = bass.bass_isa.ReduceOp.max

P = 128
N, D, F = 4096, 512, 128
KD = D // P
NT = N // P
CW = 512
NCH = N // CW
JB = CW // P
RING = 12
PT_RING = 3
XR = 3
S_BANKS, T_BANKS, U_BANKS = 3, 2, 2
EPS = 1e-5

TOP = 2.0 ** 13
TINY = 2.0 ** -40
EXP_BITS = 0x7F800000
LOGIT = 0.5 / math.sqrt(D)
P_UP = 2.0 ** 12
X1_UP = 2.0 ** 10
Y_DOWN = 2.0 ** -18

ADJ_RING = 4
AT_RING = 4
NIC = N // CW
ZB = 2
OB = 4


def gnn_program(nc, x, adj, wq, bq, wk, bk, wv, bv, w1, b1, w2, b2, out, x1_dram):
    with ExitStack() as ctx:
        def sb(name, shape, dt):
            return ctx.enter_context(nc.sbuf_tensor(name, shape, dt))

        def sem(name):
            return ctx.enter_context(nc.semaphore(name))

        xT = sb("xT", [P, 2, KD * N], F16)
        xv = sb("xv", [P, NT, D], F32)
        ring = sb("ring", [P, RING, CW], F32)
        ybuf = sb("ybuf", [P, 2, NT * F], F16)
        g_row = sb("g_row", [P, D], F32)
        gT = sb("gT", [P, 2, 2, KD * P], F16)
        pT = sb("pT", [P, PT_RING, 2, CW], F16)
        xr = sb("xr", [P, XR, D], F32)
        x1T = sb("x1T", [P, 2, KD * P], F16)
        m_hl = sb("m_hl", [P, 2, KD, D], F16)
        w1_hl = sb("w1_hl", [P, 2, KD, F], F16)
        g_bias = sb("g_bias", [P, D], F32)
        c_row = sb("c_row", [P, D], F32)
        ident = sb("ident", [P, P], F32)
        unused = sb("unused", [P, D], BF16)
        adj_max = sb("adj_max", [P, NT * NCH], F32)
        bq_c = sb("bq_c", [P, KD], F32)
        bk_c = sb("bk_c", [P, KD], F32)
        b1_c = sb("b1_c", [P, 1], F32)
        c_all = sb("c_all", [P, NT], F32)
        l_inv = sb("l_inv", [P, NT], F32)
        l_max = sb("l_max", [P, 2, NCH], F32)
        l_bias = sb("l_bias", [P, 2], F32)
        p_sum = sb("p_sum", [P, 2, NCH], F32)
        bn = sb("bn", [P, 6], F32)
        mv = sb("mv", [P, 2, 2], F32)
        veps = sb("veps", [P, 2], F32)
        rstd = sb("rstd", [P, 2], F32)
        h_max = sb("h_max", [P, NIC], F32)
        sc = sb("sc", [P, 48], F32)

        names = ["m0", "m1", "m2", "m3", "st_m", "st_wv", "st_w1", "mx_m", "mx_wv", "mx_w1", "mx_bv", "st_x", "mx_x",
                 "e_m", "e_wv", "e_w1", "e_x", "s_m", "s_wv", "s_w1", "s_x", "k_g", "k_v", "v_bound", "e_v", "s_v",
                 "k_u", "k_l", "c0", "t0", "t1", "t2", "t3", "st_a", "mx_a", "e_a", "s_a", "inv_h", "e_h", "s_h",
                 "inv_z", "minus_half"]
        col = {name: sc[:, i:i + 1] for i, name in enumerate(names)}

        def cols(first, last):
            return sc[:, names.index(first):names.index(last) + 1]

        def xt_block(part, k, tile, width=P):
            return xT[:, part, k * N + tile * P:k * N + tile * P + width]

        xt_tiles = [xT[:, part, :].rearrange("p (k n) -> p k n", k=KD) for part in range(2)]
        v_hl = xv[:, :, :].bitcast(F16).rearrange("p t (two d) -> p t two d", two=2)
        wq_raw, wk_raw, wv_raw = (ring[:, KD * i:KD * (i + 1), :] for i in range(3))
        y_flat = ybuf[:, :, :].rearrange("p a b -> p (a b)")
        wvT = y_flat[:, 0:2 * KD * D].rearrange("p (two k e) -> p two k e", two=2, k=KD)
        y_f32 = y_flat[:, 2 * KD * D:].bitcast(F32)
        bv_row, w1_raw = y_f32[:, 0:D], y_f32[:, D:2 * D].rearrange("p (k f) -> p k f", k=KD)
        v_row = [y_f32[:, (2 + i) * D:(3 + i) * D] for i in range(2)]
        y_hl = ybuf[:, :, :].rearrange("p two (t f) -> p two t f", f=F)
        adj_blk = xT[:, 0, :].bitcast(F32).rearrange("p (r t c) -> p r t c", r=ADJ_RING, t=JB)
        low = xT[:, 1, :]
        aT = low[:, 0:AT_RING * 2 * CW].rearrange("p (r two c) -> p r two c", r=AT_RING, two=2)
        hT = low[:, 4096:4096 + 2 * N].bitcast(F32)
        h_hl = xv[:, 0:8, :].bitcast(F16).rearrange("p a b -> p (a b)").rearrange("p (two t f) -> p two t f", two=2, t=NT)
        z_f = [xv[:, 8 + i, :] for i in range(ZB)]
        w2_s, b2_row = xv[:, 10, :], xv[:, 11, :]
        x1_in = [xv[:, 12 + i, :] for i in range(OB)]
        o_row = [xv[:, 16 + i, :] for i in range(OB)]

        bank = [ctx.enter_context(nc.psum_tensor(f"bank{i}", [P, CW], F32)) for i in range(8)]
        s_bank, t_bank, u_bank, misc = bank[0:3], bank[3:5], bank[5:7], bank[7]
        m_bank = [bank[0], bank[1], bank[2], bank[3]]
        wvt_bank = [bank[7], bank[4], bank[5], bank[6]]
        o_bank = [bank[5], bank[6], bank[7]]

        d_small, d_wq, d_wk, d_wv, d_late = (sem(s) for s in ("d_small", "d_wq", "d_wk", "d_wv", "d_late"))
        d_x = [sem(f"d_xgroup{i}") for i in range(NCH)]
        d_adj = [sem(f"d_adj{i}") for i in range(RING)]
        d_xr = [sem(f"d_xr{i}") for i in range(XR)]
        d_x1 = sem("d_x1")
        d_blk = [sem(f"d_blk{i}") for i in range(ADJ_RING)]
        d_x1in = [sem(f"d_x1in{i}") for i in range(OB)]
        d_out = [sem(f"d_out{i}") for i in range(OB)]
        p_pre, p_xt, p_v, p_g, p_gt = (sem(s) for s in ("p_pre", "p_xt", "p_v", "p_g", "p_gt"))
        p_qk, p_tp, p_pv, p_x1t, p_y = (sem(s) for s in ("p_qk", "p_tp", "p_pv", "p_x1t", "p_y"))
        p_at, p_am, p_ht, p_o = (sem(s) for s in ("p_at", "p_am", "p_ht", "p_o"))
        a_pre, a_xt, a_v, a_gt, a_exp, a_pt = (sem(s) for s in ("a_pre", "a_xt", "a_v", "a_gt", "a_exp", "a_pt"))
        a_x1t, a_y, a_at, a_h, a_ht, a_z = (sem(s) for s in ("a_x1t", "a_y", "a_at", "a_h", "a_ht", "a_z"))
        v_st, v_sc, v_sx, v_pre, v_xt, v_vf, v_v = (sem(s) for s in ("v_st", "v_sc", "v_sx", "v_pre", "v_xt", "v_vf", "v_v"))
        v_g, v_gt, v_add, v_bias, v_pt = (sem(s) for s in ("v_g", "v_gt", "v_add", "v_bias", "v_pt"))
        v_var, v_x1, v_x1t, v_y, v_r = (sem(s) for s in ("v_var", "v_x1", "v_x1t", "v_y", "v_r"))
        v_am, v_sa, v_at, v_h, v_ht, v_ovar, v_o, v_chain = (
            sem(s) for s in ("v_am", "v_sa", "v_at", "v_h", "v_ht", "v_ovar", "v_o", "v_chain"))
        g_id, g_ar, g_rstd, g_xb, g_orstd = (sem(s) for s in ("g_id", "g_ar", "g_rstd", "g_xb", "g_orstd"))

        block = ctx.enter_context(nc.Block())

        def load_block(sp, q):
            ic, jq = divmod(q % (NIC * NCH), NCH)
            sp.dma_start(adj_blk[:, q % ADJ_RING, :, :],
                         adj[CW * ic:CW * (ic + 1), CW * jq:CW * (jq + 1)].rearrange("(t p) c -> p t c", p=P)
                         ).then_inc(d_blk[q % ADJ_RING], 16)

        def load_x1(sp, t):
            sp.dma_start(x1_in[t % OB], x1_dram[P * t:P * (t + 1), :]).then_inc(d_x1in[t % OB], 16)

        def store_out(sp, t):
            sp.wait_ge(v_o, t + 1)
            sp.dma_start(out[P * t:P * (t + 1), :], o_row[t % OB]).then_inc(d_out[t % OB], 16)
            if t + OB < NT:
                load_x1(sp, t + OB)

        @block.sync
        def _(sp):
            sp.dma_start(bq_c[:, :], bq.rearrange("(p k) -> p k", k=KD)).then_inc(d_small, 16)
            sp.dma_start(bk_c[:, :], bk.rearrange("(p k) -> p k", k=KD)).then_inc(d_small, 16)
            sp.dma_start(b1_c[:, :], b1.rearrange("(p o) -> p o", o=1)).then_inc(d_small, 16)
            sp.dma_start(wq_raw, wq.rearrange("(p k) d -> p k d", k=KD)).then_inc(d_wq, 16)
            sp.dma_start(wk_raw, wk.rearrange("(p k) d -> p k d", k=KD)).then_inc(d_wk, 16)
            sp.dma_start(wv_raw, wv.rearrange("(k p) d -> p k d", p=P)).then_inc(d_wv, 16)
            sp.dma_start(bv_row, bv.rearrange("(o d) -> o d", o=1).broadcast_to([P, D])).then_inc(d_small, 16)
            sp.dma_start(w1_raw, w1.rearrange("(k p) f -> p k f", p=P)).then_inc(d_small, 16)
            x_tiles = x.rearrange("(t p) d -> p t d", p=P)
            for i in range(NCH):
                sp.dma_start(xv[:, JB * i:JB * (i + 1), :], x_tiles[:, JB * i:JB * (i + 1), :]).then_inc(d_x[i], 16)
            for t in range(XR):
                sp.dma_start(xr[:, t, :], x_tiles[:, t, :]).then_inc(d_xr[t], 16)

            def load_adj(n):
                t, c = divmod(n, NCH)
                sp.dma_start(ring[:, n % RING, :], adj[P * t:P * (t + 1), CW * c:CW * (c + 1)]).then_inc(d_adj[n % RING], 16)

            sp.wait_ge(p_pre, 7)
            for n in range(2 * KD):
                load_adj(n)
            sp.wait_ge(p_pre, 11)
            sp.wait_ge(v_st, 3)
            for n in range(2 * KD, RING):
                load_adj(n)
            for t in range(NT + 1):
                for c in range(NCH):
                    n = NCH * t + c
                    if n + RING < NT * NCH:
                        sp.wait_ge(p_tp, n + 1)
                        load_adj(n + RING)
                    if c == 4 and t >= 1:
                        sp.wait_ge(v_x1, t)
                        sp.dma_start(x1_dram[P * (t - 1):P * t, :], xr[:, (t - 1) % XR, :]).then_inc(d_x1, 16)
                    if c == 7 and t >= 1 and t + 2 < NT:
                        sp.wait_ge(d_x1, 16 * t)
                        sp.wait_ge(p_x1t, t)
                        sp.dma_start(xr[:, (t + 2) % XR, :], x_tiles[:, t + 2, :]).then_inc(d_xr[(t + 2) % XR], 16)
                if t == NT - 1:
                    sp.wait_ge(p_qk, NT * NCH)
                    for q in range(ADJ_RING):
                        load_block(sp, q)
            for q in range(ADJ_RING, 2 * NIC * NCH):
                sp.wait_ge(p_at, JB * (q - ADJ_RING + 1))
                load_block(sp, q)
                if q == ADJ_RING:
                    sp.wait_ge(p_pv, NT * NCH)
                    sp.dma_start(w2_s, w2[:, :]).then_inc(d_late, 16)
                    sp.dma_start(b2_row, b2.rearrange("(o d) -> o d", o=1).broadcast_to([P, D])).then_inc(d_late, 16)
                    sp.wait_ge(d_x1, 16 * NT)
                    for i in range(OB):
                        load_x1(sp, i)
                i, step = divmod(q - NIC * NCH, NCH)
                if i >= 1 and step in (2, 4, 6, 7):
                    store_out(sp, JB * (i - 1) + (2, 4, 6, 7).index(step))
            for t in range(NT - JB, NT):
                store_out(sp, t)
            for i in range(OB):
                sp.wait_ge(d_out[i], 16 * (NT // OB))

        def product(pe, dst, pairs):
            for i, (ah, al, bh, bl) in enumerate(pairs):
                pe.matmul(dst, ah, bh, start=(i == 0), stop=False)
                pe.matmul(dst, ah, bl, start=False, stop=False)
                last = pe.matmul(dst, al, bh, start=False, stop=(i == len(pairs) - 1))
            return last

        @block.tensor
        def _(pe):
            pe.wait_ge(g_id, 2)
            pe.wait_ge(d_small, 16 * 5)
            pe.wait_ge(d_wq, 16)
            pe.wait_ge(d_wk, 16)
            for k in range(KD):
                for e in range(KD):
                    last = pe.matmul(m_bank[k][:, :], wq_raw[:, e, P * k:P * (k + 1)], wk_raw[:, e, :],
                                     start=(e == 0), stop=(e == KD - 1))
                last.then_inc(p_pre, 1)

            def row_of(dst, vec, mat):
                for e in range(KD):
                    last = pe.matmul(dst, vec[:, e:e + 1].broadcast_to([P, P]), mat(e), start=(e == 0), stop=(e == KD - 1))
                last.then_inc(p_pre, 1)

            row_of(bank[4][:, :], bq_c, lambda e: wk_raw[:, e, :])
            row_of(bank[5][:, :], bk_c, lambda e: wq_raw[:, e, :])
            row_of(bank[6][:, 0:1], bq_c, lambda e: bk_c[:, e:e + 1])
            pe.wait_ge(d_wv, 16)
            pe.wait_ge(v_pre, 3)
            for k in range(KD):
                for e in range(KD):
                    last = pe.transpose(wvt_bank[k][:, P * e:P * (e + 1)], wv_raw[:, e, P * k:P * (k + 1)], ident[:, :])
                last.then_inc(p_pre, 1)
            pe.wait_ge(a_pre, 2 * KD)
            pe.wait_ge(v_pre, 3 + 2 * KD)

            def x_transpose(t):
                pe.wait_ge(d_x[t // JB], 16)
                if t >= T_BANKS:
                    pe.wait_ge(a_xt, t - T_BANKS + 1)
                    pe.wait_ge(v_xt, t - T_BANKS + 1)
                for k in range(KD):
                    last = pe.transpose(t_bank[t % T_BANKS][:, P * k:P * (k + 1)], xv[:, t, P * k:P * (k + 1)], ident[:, :])
                last.then_inc(p_xt, 1)

            def v_rows(t):
                pe.wait_ge(a_xt, t + 1)
                pe.wait_ge(v_xt, t + 1)
                if t >= U_BANKS:
                    pe.wait_ge(v_vf, t - U_BANKS + 1)
                product(pe, u_bank[t % U_BANKS][:, :],
                        [(xt_block(0, k, t), xt_block(1, k, t), wvT[:, 0, k, :], wvT[:, 1, k, :]) for k in range(KD)]
                        ).then_inc(p_v, 1)

            done = {"g": 0, "y": 0}

            def misc_free():
                if done["g"]:
                    pe.wait_ge(a_gt, done["g"])
                    pe.wait_ge(v_gt, done["g"])
                if done["y"]:
                    pe.wait_ge(a_y, done["y"])
                    pe.wait_ge(v_y, done["y"])

            def g_rows(t):
                misc_free()
                product(pe, misc[:, :],
                        [(xt_block(0, k, t), xt_block(1, k, t), m_hl[:, 0, k, :], m_hl[:, 1, k, :]) for k in range(KD)]
                        ).then_inc(p_g, 1)

            def g_transpose(t):
                pe.wait_ge(v_g, t + 1)
                for k in range(KD):
                    last = pe.transpose(misc[:, P * k:P * (k + 1)], g_row[:, P * k:P * (k + 1)], ident[:, :])
                last.then_inc(p_gt, 1)
                done["g"] += 1

            def logits(n):
                t, c = divmod(n, NCH)
                pe.wait_ge(a_gt, t + 1)
                pe.wait_ge(v_gt, t + 1)
                if n >= S_BANKS:
                    pe.wait_ge(v_add, n - S_BANKS + 1)
                a = gT[:, t % 2, :, :]
                product(pe, s_bank[n % S_BANKS][:, :],
                        [(a[:, 0, P * k:P * (k + 1)], a[:, 1, P * k:P * (k + 1)],
                          xt_block(0, k, JB * c, CW), xt_block(1, k, JB * c, CW)) for k in range(KD)]
                        ).then_inc(p_qk, 1)

            def p_transpose(n):
                pe.wait_ge(a_exp, n + 1)
                if n >= T_BANKS:
                    pe.wait_ge(a_pt, n - T_BANKS + 1)
                    pe.wait_ge(v_pt, n - T_BANKS + 1)
                for b in range(JB):
                    last = pe.transpose(t_bank[n % T_BANKS][:, P * b:P * (b + 1)],
                                        ring[:, n % RING, P * b:P * (b + 1)], ident[:, :])
                last.then_inc(p_tp, 1)

            def attend(n):
                t, c = divmod(n, NCH)
                pe.wait_ge(a_pt, n + 1)
                pe.wait_ge(v_pt, n + 1)
                if c == 0 and t >= U_BANKS:
                    pe.wait_ge(v_r, t - U_BANKS + 1)
                dst = u_bank[t % U_BANKS][:, :]
                a = pT[:, n % PT_RING, :, :]
                for b in range(JB):
                    ah, al = a[:, 0, P * b:P * (b + 1)], a[:, 1, P * b:P * (b + 1)]
                    vh, vl = v_hl[:, JB * c + b, 0, :], v_hl[:, JB * c + b, 1, :]
                    pe.matmul(dst, ah, vh, start=(c == 0 and b == 0), stop=False)
                    pe.matmul(dst, ah, vl, start=False, stop=False)
                    last = pe.matmul(dst, al, vh, start=False, stop=(c == NCH - 1 and b == JB - 1))
                last.then_inc(p_pv, 1)

            def x1_transpose(t):
                misc_free()
                pe.wait_ge(v_x1, t + 1)
                for k in range(KD):
                    last = pe.transpose(misc[:, P * k:P * (k + 1)], xr[:, t % XR, P * k:P * (k + 1)], ident[:, :])
                last.then_inc(p_x1t, 1)

            def y_rows(t):
                pe.wait_ge(a_x1t, t + 1)
                pe.wait_ge(v_x1t, t + 1)
                product(pe, misc[:, 0:F],
                        [(x1T[:, 0, P * k:P * (k + 1)], x1T[:, 1, P * k:P * (k + 1)], w1_hl[:, 0, k, :], w1_hl[:, 1, k, :])
                         for k in range(KD)]).then_inc(p_y, 1)
                done["y"] += 1

            x_transpose(0)
            for t in range(NT):
                if t + 1 < NT:
                    x_transpose(t + 1)
                v_rows(t)
                if t == 0:
                    g_rows(0)
                elif t == 2:
                    g_transpose(0)
                elif t == 5:
                    g_rows(1)
                elif t == 8:
                    g_transpose(1)
                if t % JB == JB - 1:
                    logits(t // JB)
            pe.wait_ge(v_vf, NT)
            pe.wait_ge(a_xt, NT)
            pe.wait_ge(v_xt, NT)
            pe.wait_ge(a_v, NT)
            pe.wait_ge(v_v, NT)
            for t in range(NT):
                for c in range(NCH):
                    n = NCH * t + c
                    if t + 1 < NT:
                        logits(n + NCH)
                    p_transpose(n)
                    if c == 1 and t + 2 < NT:
                        g_rows(t + 2)
                    if c == 4 and t + 2 < NT:
                        g_transpose(t + 2)
                    if c == 5 and t >= 1:
                        x1_transpose(t - 1)
                    if c == 6 and t >= 1:
                        y_rows(t - 1)
                    if n >= 1:
                        attend(n - 1)
            attend(NT * NCH - 1)

            def a_transpose(m):
                q, b = divmod(m, JB)
                if b == 0:
                    pe.wait_ge(d_blk[q % ADJ_RING], 16 * (q // ADJ_RING + 1))
                if m >= S_BANKS:
                    pe.wait_ge(a_at, m - S_BANKS + 1)
                    pe.wait_ge(v_at, m - S_BANKS + 1)
                else:
                    pe.wait_ge(v_add, NT * NCH)
                for t in range(JB):
                    last = pe.transpose(s_bank[m % S_BANKS][:, P * t:P * (t + 1)],
                                        adj_blk[:, q % ADJ_RING, t, P * b:P * (b + 1)], ident[:, :])
                last.then_inc(p_at, 1)

            def a_product(m):
                i, jb = divmod(m, NT)
                dst = t_bank[i % 2][:, :]
                pe.wait_ge(a_at, m + 1)
                pe.wait_ge(v_at, m + 1)
                if jb == 0 and 2 <= i < NIC:
                    pe.wait_ge(a_h, i - 1)
                if jb == 0 and i in (NIC, NIC + 1):
                    pe.wait_ge(a_h, i - 1)
                if jb == 0 and i >= NIC + 2:
                    pe.wait_ge(a_z, i - NIC - 1)
                s = y_hl if i < NIC else h_hl
                if i == NIC and jb % JB == 0:
                    pe.wait_ge(a_ht, jb // JB + 1)
                    pe.wait_ge(v_ht, jb // JB + 1)
                ah, al = aT[:, m % AT_RING, 0, :], aT[:, m % AT_RING, 1, :]
                pe.matmul(dst, s[:, 0, jb, :], ah, start=(jb == 0), stop=False)
                pe.matmul(dst, s[:, 0, jb, :], al, start=False, stop=False)
                last = pe.matmul(dst, s[:, 1, jb, :], ah, start=False, stop=(jb == NT - 1))
                last.then_inc(p_am, 1)

            def h_transpose(g):
                pe.wait_ge(v_h, g + 1)
                if g >= 3:
                    pe.wait_ge(a_ht, g - 2)
                    pe.wait_ge(v_ht, g - 2)
                for b in range(JB):
                    last = pe.transpose(o_bank[g % 3][:, P * b:P * (b + 1)],
                                        hT[:, CW * g + P * b:CW * g + P * (b + 1)], ident[:, :])
                last.then_inc(p_ht, 1)

            def o_rows(t):
                i, b = divmod(t, JB)
                if b == 0:
                    pe.wait_ge(a_z, i + 1)
                if t >= 3:
                    pe.wait_ge(v_ovar, t - 2)
                pe.matmul(o_bank[t % 3][:, :], z_f[i % ZB][:, P * b:P * (b + 1)], w2_s, start=True, stop=True).then_inc(p_o, 1)

            AHEAD = 2
            for m in range(AHEAD):
                a_transpose(m)
            x1_transpose(NT - 1)
            y_rows(NT - 1)
            pe.wait_ge(a_y, NT)
            pe.wait_ge(v_y, NT)
            steps = 2 * NIC * NT
            for m in range(steps):
                if m + AHEAD < steps:
                    a_transpose(m + AHEAD)
                if m == NIC * NT:
                    for g in range(NCH):
                        h_transpose(g)
                    pe.wait_ge(a_ht, NCH)
                    pe.wait_ge(v_ht, NCH)
                    pe.wait_ge(d_late, 32)
                a_product(m)
                i, jb = divmod(m - NIC * NT, NT)
                if i >= 1 and jb in (4, 10, 16, 22):
                    o_rows(JB * (i - 1) + (4, 10, 16, 22).index(jb))
            for t in range(NT - JB, NT):
                o_rows(t)

        def h_out(act, i):
            act.wait_ge(p_am, NT * (i + 1))
            act.activation(hT[:, CW * i:CW * (i + 1)], t_bank[i % 2][:, :], ACT.Relu, bias=b1_c[:, :],
                           scale=col["inv_h"]).then_inc(a_h, 1)

        def z_out(act, i):
            act.wait_ge(p_am, NT * (NIC + i + 1))
            if i >= ZB:
                act.wait_ge(p_o, JB * (i - ZB + 1))
            act.activation(z_f[i % ZB], t_bank[i % 2][:, :], ACT.Copy, scale=col["inv_z"]).then_inc(a_z, 1)

        @block.scalar
        def _(act):
            act.wait_ge(v_sc, 1)
            for k in range(KD):
                act.wait_ge(p_pre, 1 + k)
                act.activation(m_hl[:, 0, k, :], m_bank[k][:, :], ACT.Identity, scale=col["s_m"]).then_inc(a_pre, 1)
            for k in range(KD):
                act.wait_ge(p_pre, 8 + k)
                act.activation(wvT[:, 0, k, :], wvt_bank[k][:, :], ACT.Identity, scale=col["s_wv"]).then_inc(a_pre, 1)
            act.activation(w1_hl[:, 0, :, :], w1_raw, ACT.Identity, scale=col["s_w1"]).then_inc(a_pre, 1)

            def xt_hi(t):
                act.wait_ge(p_xt, t + 1)
                act.activation(xt_tiles[0][:, :, P * t:P * (t + 1)],
                               t_bank[t % T_BANKS][:, :].rearrange("p (k n) -> p k n", k=KD),
                               ACT.Identity, scale=col["s_x"]).then_inc(a_xt, 1)

            def g_hi(t):
                act.wait_ge(p_gt, t + 1)
                if t >= 2:
                    act.wait_ge(p_qk, NCH * (t - 1))
                act.activation(gT[:, t % 2, 0, :], misc[:, :], ACT.Copy).then_inc(a_gt, 1)

            act.wait_ge(v_sx, 1)
            xt_hi(0)
            for t in range(NT):
                if t + 1 < NT:
                    xt_hi(t + 1)
                act.wait_ge(v_vf, t + 1)
                act.activation(v_hl[:, t, 0, :], v_row[t % 2], ACT.Identity, scale=col["s_v"]).then_inc(a_v, 1)
                if t == 2:
                    g_hi(0)
                if t == 8:
                    g_hi(1)

            def exp(n):
                t, c = divmod(n, NCH)
                if c == 0:
                    act.wait_ge(v_bias, t + 1)
                act.activation(ring[:, n % RING, :], ring[:, n % RING, :], ACT.Exp, bias=l_bias[:, t % 2:t % 2 + 1],
                               scale=2.0, accum_out=p_sum[:, t % 2, c:c + 1]).then_inc(a_exp, 1)

            def pt_hi(n):
                act.wait_ge(p_tp, n + 1)
                if n >= PT_RING:
                    act.wait_ge(p_pv, n - PT_RING + 1)
                act.activation(pT[:, n % PT_RING, 0, :], t_bank[n % T_BANKS][:, :], ACT.Copy, scale=P_UP).then_inc(a_pt, 1)

            def x1_hi(t):
                act.wait_ge(p_x1t, t + 1)
                if t >= 1:
                    act.wait_ge(p_y, t)
                act.activation(x1T[:, 0, :], misc[:, :], ACT.Copy, scale=X1_UP).then_inc(a_x1t, 1)

            def y_hi(t):
                act.wait_ge(p_y, t + 1)
                act.activation(y_hl[:, 0, t, :], misc[:, 0:F], ACT.Copy, scale=Y_DOWN).then_inc(a_y, 1)

            for t in range(NT):
                for c in range(NCH):
                    n = NCH * t + c
                    if c == 0:
                        exp(n)
                    if c + 1 < NCH:
                        exp(n + 1)
                    pt_hi(n)
                    if c == 4 and t + 2 < NT:
                        g_hi(t + 2)
                    if c == 5 and t >= 1:
                        x1_hi(t - 1)
                    if c == 7 and t >= 1:
                        y_hi(t - 1)
            x1_hi(NT - 1)
            y_hi(NT - 1)

            act.wait_ge(v_sa, 1)
            for m in range(2 * NIC * NT):
                act.wait_ge(p_at, m + 1)
                if m >= AT_RING:
                    act.wait_ge(p_am, m - AT_RING + 1)
                act.activation(aT[:, m % AT_RING, 0, :], s_bank[m % S_BANKS][:, :], ACT.Copy,
                               scale=col["s_a"]).then_inc(a_at, 1)
                i, jb = divmod(m, NT)
                if jb == 1 and 1 <= i < NIC:
                    h_out(act, i - 1)
                if i == NIC and jb == 1:
                    h_out(act, NIC - 1)
                    for g in range(NCH):
                        act.wait_ge(p_ht, g + 1)
                        act.activation(h_hl[:, 0, JB * g:JB * (g + 1), :],
                                       o_bank[g % 3][:, :].rearrange("p (t f) -> p t f", f=F), ACT.Copy).then_inc(a_ht, 1)
                if jb == 1 and i > NIC:
                    z_out(act, i - NIC - 1)
            z_out(act, NIC - 1)

        @block.vector
        def _(dve):
            chained = [0]

            def link(ins):
                chained[0] += 1
                ins.then_inc(v_chain, 1)
                dve.wait_ge(v_chain, chained[0])

            def abs_max(dst, src):
                return dve.tensor_reduce(dst, src, AX, ALU.max, apply_absolute_value=True)

            def power(dst, src):
                link(dve.tensor_scalar(dst, src, TINY, None, ALU.max))
                link(dve.tensor_scalar(dst.bitcast(U32), dst.bitcast(U32), EXP_BITS, None, ALU.bitwise_and))

            def scale_of(dst, power_of):
                link(dve.reciprocal(dst, power_of))
                link(dve.tensor_scalar(dst, dst, TOP, None, ALU.mult))

            def minus_hi(dst, src, scale, hi):
                return dve.scalar_tensor_tensor(dst, src, scale, hi, ALU.mult, ALU.subtract)

            def x_max(i):
                dve.wait_ge(d_x[i], 16)
                abs_max(l_max_x[:, i:i + 1], xv[:, JB * i:JB * (i + 1), :].rearrange("p a b -> p (a b)")).then_inc(v_am, 1)

            l_max_x = l_max[:, 0, :]
            dve.wait_ge(d_wv, 16)
            dve.wait_ge(d_small, 16 * 5)
            abs_max(col["st_wv"], wv_raw.rearrange("p k d -> p (k d)")).then_inc(v_st, 1)
            abs_max(col["st_w1"], w1_raw.rearrange("p k f -> p (k f)")).then_inc(v_st, 1)
            abs_max(col["mx_bv"], bv_row).then_inc(v_st, 1)
            for i in range(4):
                x_max(i)
            dve.wait_ge(p_pre, 7)
            for k in range(KD):
                link(abs_max(col[f"m{k}"], m_bank[k][:, :]))
            dve.tensor_reduce(col["st_m"], cols("m0", "m3"), AX, ALU.max).then_inc(v_st, 1)
            dve.tensor_scalar(g_bias[:, :], bank[4][:, :], LOGIT, None, ALU.mult).then_inc(v_pre, 1)
            dve.tensor_copy(c_row[:, :], bank[5][:, :]).then_inc(v_pre, 1)
            dve.tensor_copy(col["c0"], bank[6][:, 0:1]).then_inc(v_pre, 1)
            for i in range(4, 6):
                x_max(i)
            dve.wait_ge(g_ar, 1)
            power(cols("e_m", "e_w1"), cols("mx_m", "mx_w1"))
            link(dve.reciprocal(cols("s_m", "s_w1"), cols("e_m", "e_w1")))
            dve.tensor_scalar(cols("s_m", "s_w1"), cols("s_m", "s_w1"), TOP, None, ALU.mult).then_inc(v_sc, 1)
            for k in range(KD):
                dve.wait_ge(a_pre, 1 + k)
                minus_hi(m_hl[:, 1, k, :], m_bank[k][:, :], col["s_m"], m_hl[:, 0, k, :]).then_inc(v_pre, 1)
            for k in range(KD):
                dve.wait_ge(a_pre, 1 + KD + k)
                minus_hi(wvT[:, 1, k, :], wvt_bank[k][:, :], col["s_wv"], wvT[:, 0, k, :]).then_inc(v_pre, 1)
            dve.wait_ge(a_pre, 1 + 2 * KD)
            minus_hi(w1_hl[:, 1, :, :].rearrange("p k f -> p (k f)"), w1_raw.rearrange("p k f -> p (k f)"), col["s_w1"],
                     w1_hl[:, 0, :, :].rearrange("p k f -> p (k f)")).then_inc(v_pre, 1)
            for i in range(6, NCH):
                x_max(i)
            dve.wait_ge(v_am, NCH)
            dve.tensor_reduce(col["st_x"], l_max_x, AX, ALU.max).then_inc(v_st, 1)
            dve.wait_ge(g_ar, 2)
            power(col["e_x"], col["mx_x"])
            scale_of(col["s_x"], col["e_x"])
            link(dve.tensor_scalar(col["k_g"], col["e_x"], col["e_m"], LOGIT / TOP ** 2, ALU.mult, ALU.mult))
            link(dve.tensor_scalar(col["k_v"], col["e_x"], col["e_wv"], 1 / TOP ** 2, ALU.mult, ALU.mult))
            link(dve.tensor_scalar(col["k_l"], col["e_x"], 1 / TOP ** 2, None, ALU.mult))
            link(dve.tensor_scalar(col["v_bound"], col["k_v"], 4.0 * D * TOP ** 2, col["mx_bv"], ALU.mult, ALU.add))
            power(col["e_v"], col["v_bound"])
            scale_of(col["s_v"], col["e_v"])
            dve.tensor_scalar(col["k_u"], col["e_v"], 1 / (TOP * P_UP), None, ALU.mult).then_inc(v_sx, 1)
            dve.wait_ge(v_sx, 1)

            def xt_lo(t):
                dve.wait_ge(a_xt, t + 1)
                minus_hi(xt_tiles[1][:, :, P * t:P * (t + 1)], t_bank[t % T_BANKS][:, :].rearrange("p (k n) -> p k n", k=KD),
                         col["s_x"], xt_tiles[0][:, :, P * t:P * (t + 1)]).then_inc(v_xt, 1)

            def c_of(t):
                dve.wait_ge(d_xr[t % XR], 16 * (t // XR + 1))
                link(dve.tensor_tensor_reduce(unused[:, :], xr[:, t % XR, :], c_row[:, :], 1.0, 0.0, ALU.mult, ALU.add,
                                              col["t3"]))
                link(dve.tensor_scalar(c_all[:, t:t + 1], col["t3"], col["c0"], LOGIT, ALU.add, ALU.mult))

            def g_scale(t):
                dve.wait_ge(p_g, t + 1)
                if t >= 1:
                    dve.wait_ge(p_gt, t)
                link(dve.scalar_tensor_tensor(g_row[:, :], misc[:, :], col["k_g"], g_bias[:, :], ALU.mult, ALU.add))
                link(abs_max(col["t0"], g_row[:, :]))
                power(col["t1"], col["t0"])
                scale_of(col["t2"], col["t1"])
                link(dve.tensor_scalar(l_inv[:, t:t + 1], col["t1"], col["k_l"], None, ALU.mult))
                dve.tensor_scalar(g_row[:, :], g_row[:, :], col["t2"], None, ALU.mult).then_inc(v_g, 1)

            def g_lo(t):
                dve.wait_ge(a_gt, t + 1)
                minus_hi(gT[:, t % 2, 1, :], misc[:, :], 1.0, gT[:, t % 2, 0, :]).then_inc(v_gt, 1)

            def adj_maximum(n):
                dve.wait_ge(d_adj[n % RING], 16 * (n // RING + 1))
                abs_max(adj_max[:, n:n + 1], ring[:, n % RING, :])

            def add_adj(n):
                t = n // NCH
                dve.wait_ge(p_qk, n + 1)
                dve.scalar_tensor_tensor(ring[:, n % RING, :], s_bank[n % S_BANKS][:, :], l_inv[:, t:t + 1],
                                         ring[:, n % RING, :], ALU.mult, ALU.add).then_inc(v_add, 1)

            def chunk_max(n):
                t, c = divmod(n, NCH)
                dve.wait_ge(v_add, n + 1)
                ins = dve.tensor_reduce(l_max[:, t % 2, c:c + 1], ring[:, n % RING, :], AX, ALU.max)
                if c == NCH - 1:
                    link(ins)

            def row_bias(t):
                link(dve.tensor_reduce(col["t0"], l_max[:, t % 2, :], AX, ALU.max))
                link(dve.tensor_tensor(col["t1"], col["t0"], c_all[:, t:t + 1], ALU.add))
                dve.tensor_scalar(l_bias[:, t % 2:t % 2 + 1], col["t1"], c_all[:, t:t + 1], -2.0,
                                  ALU.subtract, ALU.mult).then_inc(v_bias, 1)

            def pt_lo(n):
                dve.wait_ge(a_pt, n + 1)
                minus_hi(pT[:, n % PT_RING, 1, :], t_bank[n % T_BANKS][:, :], P_UP, pT[:, n % PT_RING, 0, :]).then_inc(v_pt, 1)

            def attention_rows(t):
                r = xr[:, t % XR, :]
                dve.wait_ge(p_pv, NCH * (t + 1))
                link(dve.tensor_reduce(col["t0"], p_sum[:, t % 2, :], AX, ALU.add))
                link(dve.reciprocal(col["t1"], col["t0"]))
                link(dve.tensor_scalar(col["t1"], col["t1"], col["k_u"], None, ALU.mult))
                dve.scalar_tensor_tensor(r, u_bank[t % U_BANKS][:, :], col["t1"], r, ALU.mult, ALU.add).then_inc(v_r, 1)
                dve.wait_ge(v_r, t + 1)
                link(dve.bn_stats(bn[:, :], r))
                link(dve.bn_aggr(mv[:, t % 2, :], bn[:, :]))
                dve.tensor_scalar(veps[:, t % 2:t % 2 + 1], mv[:, t % 2, 1:2], EPS, None, ALU.add).then_inc(v_var, 1)

            def normalise(t):
                dve.wait_ge(g_rstd, t + 1)
                dve.tensor_scalar(xr[:, t % XR, :], xr[:, t % XR, :], mv[:, t % 2, 0:1], rstd[:, t % 2:t % 2 + 1],
                                  ALU.subtract, ALU.mult).then_inc(v_x1, 1)

            def x1_lo(t):
                dve.wait_ge(a_x1t, t + 1)
                minus_hi(x1T[:, 1, :], misc[:, :], X1_UP, x1T[:, 0, :]).then_inc(v_x1t, 1)

            def y_lo(t):
                dve.wait_ge(a_y, t + 1)
                minus_hi(y_hl[:, 1, t, :], misc[:, 0:F], Y_DOWN, y_hl[:, 0, t, :]).then_inc(v_y, 1)

            xt_lo(0)
            c_of(0)
            for t in range(NT):
                if t + 1 < NT:
                    xt_lo(t + 1)
                dve.wait_ge(p_v, t + 1)
                if t >= 2:
                    dve.wait_ge(a_v, t - 1)
                dve.scalar_tensor_tensor(v_row[t % 2], u_bank[t % U_BANKS][:, :], col["k_v"], bv_row,
                                         ALU.mult, ALU.add).then_inc(v_vf, 1)
                if t == 0:
                    g_scale(0)
                elif t == 2:
                    g_lo(0)
                elif t == 6:
                    g_scale(1)
                elif t == 8:
                    g_lo(1)
                dve.wait_ge(a_v, t + 1)
                dve.wait_ge(v_vf, t + 1)
                minus_hi(v_hl[:, t, 1, :], v_row[t % 2], col["s_v"], v_hl[:, t, 0, :]).then_inc(v_v, 1)
                if t % JB == JB - 1:
                    n = t // JB
                    adj_maximum(n)
                    add_adj(n)
                    chunk_max(n)
            row_bias(0)
            for t in range(NT):
                for c in range(NCH):
                    n = NCH * t + c
                    if t + 1 < NT:
                        adj_maximum(n + NCH)
                        add_adj(n + NCH)
                    pt_lo(n)
                    if t + 1 < NT:
                        chunk_max(n + NCH)
                    if c == 1 and t >= 1:
                        attention_rows(t - 1)
                    if c == 2 and t + 2 < NT:
                        g_scale(t + 2)
                    if c == 3 and t >= 1:
                        normalise(t - 1)
                    if c == 4 and t + 2 < NT:
                        g_lo(t + 2)
                    if c == 5 and t >= 1:
                        x1_lo(t - 1)
                    if c == 6 and t + 1 < NT:
                        c_of(t + 1)
                    if c == 7 and t >= 1:
                        y_lo(t - 1)
                if t + 1 < NT:
                    row_bias(t + 1)
                if t == NT - 2:
                    dve.tensor_reduce(col["st_a"], adj_max[:, :], AX, ALU.max).then_inc(v_st, 1)
                if t == NT - 1:
                    dve.wait_ge(g_ar, 3)
                    power(col["e_a"], col["mx_a"])
                    scale_of(col["s_a"], col["e_a"])
                    dve.tensor_scalar(col["inv_h"], col["e_a"], col["e_w1"], 1 / (TOP * TOP * X1_UP * Y_DOWN),
                                      ALU.mult, ALU.mult).then_inc(v_sa, 1)
            attention_rows(NT - 1)
            normalise(NT - 1)
            x1_lo(NT - 1)
            y_lo(NT - 1)

            def o_stats(t):
                dve.wait_ge(p_o, t + 1)
                dve.wait_ge(g_xb, t + 1)
                if t >= OB:
                    dve.wait_ge(d_out[t % OB], 16 * (t // OB))
                dve.tensor_tensor(o_row[t % OB], o_bank[t % 3][:, :], x1_in[t % OB], ALU.add).then_inc(v_ovar, 1)
                dve.wait_ge(v_ovar, t + 1)
                link(dve.bn_stats(bn[:, :], o_row[t % OB]))
                link(dve.bn_aggr(mv[:, t % 2, :], bn[:, :]))
                dve.tensor_scalar(veps[:, t % 2:t % 2 + 1], mv[:, t % 2, 1:2], EPS, None, ALU.add).then_inc(v_var, 1)

            def o_normalise(t):
                dve.wait_ge(g_rstd, NT + t + 1)
                dve.tensor_scalar(o_row[t % OB], o_row[t % OB], mv[:, t % 2, 0:1], rstd[:, t % 2:t % 2 + 1],
                                  ALU.subtract, ALU.mult).then_inc(v_o, 1)

            for m in range(2 * NIC * NT):
                dve.wait_ge(a_at, m + 1)
                minus_hi(aT[:, m % AT_RING, 1, :], s_bank[m % S_BANKS][:, :], col["s_a"], aT[:, m % AT_RING, 0, :]).then_inc(v_at, 1)
                i, jb = divmod(m, NT)
                if jb == 1 and 1 <= i <= NIC:
                    dve.wait_ge(a_h, i)
                    link(abs_max(h_max[:, i - 1:i], hT[:, CW * (i - 1):CW * i]))
                if jb == 1 and i == NIC:
                    link(dve.tensor_reduce(col["t0"], h_max[:, :], AX, ALU.max))
                    power(col["e_h"], col["t0"])
                    scale_of(col["s_h"], col["e_h"])
                    link(dve.tensor_scalar(col["inv_z"], col["e_h"], col["e_a"], 1 / TOP ** 2, ALU.mult, ALU.mult))
                    for g in range(NCH):
                        dve.tensor_scalar(hT[:, CW * g:CW * (g + 1)], hT[:, CW * g:CW * (g + 1)], col["s_h"], None,
                                          ALU.mult).then_inc(v_h, 1)
                    for g in range(NCH):
                        dve.wait_ge(a_ht, g + 1)
                        minus_hi(h_hl[:, 1, JB * g:JB * (g + 1), :].rearrange("p t f -> p (t f)"), o_bank[g % 3][:, :], 1.0,
                                 h_hl[:, 0, JB * g:JB * (g + 1), :].rearrange("p t f -> p (t f)")).then_inc(v_ht, 1)
                if i > NIC:
                    t0 = JB * (i - NIC - 1)
                    if jb in (6, 12, 18, 24):
                        o_stats(t0 + (6, 12, 18, 24).index(jb))
                    if jb in (8, 14, 20, 26):
                        o_normalise(t0 + (8, 14, 20, 26).index(jb))
            for t in range(NT - JB, NT):
                o_stats(t)
                o_normalise(t)

        @block.gpsimd
        def _(pool):
            pool.memset(ident[:, :], 0.0).then_inc(g_id, 1)
            pool.memset(col["minus_half"], -0.5)
            pool.wait_ge(g_id, 1)
            pool.affine_select(out=ident[:, :], in_=ident[:, :], compare_op=ALU.not_equal, fill=1.0, base=0,
                               pattern=[[-1, P]], channel_multiplier=1).then_inc(g_id, 1)
            pool.wait_ge(v_st, 4)
            pool.partition_all_reduce(cols("mx_m", "mx_w1"), cols("st_m", "st_w1"), P, ALL_MAX).then_inc(g_ar, 1)
            pool.wait_ge(v_st, 5)
            pool.partition_all_reduce(col["mx_x"], col["st_x"], P, ALL_MAX).then_inc(g_ar, 1)

            def root(t):
                pool.wait_ge(v_var, t + 1)
                pool.tensor_tensor(rstd[:, t % 2:t % 2 + 1], veps[:, t % 2:t % 2 + 1], col["minus_half"],
                                   ALU.pow).then_inc(g_rstd, 1)

            for t in range(NT - 2):
                root(t)
            pool.wait_ge(v_st, 6)
            pool.partition_all_reduce(col["mx_a"], col["st_a"], P, ALL_MAX).then_inc(g_ar, 1)
            root(NT - 2)
            root(NT - 1)
            pool.wait_ge(d_late, 32)
            for t in range(NT):
                pool.wait_ge(d_x1in[t % OB], 16 * (t // OB + 1))
                pool.tensor_tensor(x1_in[t % OB], x1_in[t % OB], b2_row, ALU.add).then_inc(g_xb, 1)
                if t >= 2:
                    root(NT + t - 2)
            root(2 * NT - 2)
            root(2 * NT - 1)


_INPUTS = ["x", "adj", "L0_gnn_Wq", "L0_gnn_bq", "L0_gnn_Wk", "L0_gnn_bk", "L0_gnn_Wv", "L0_gnn_bv",
           "L1_gnn_W1", "L1_gnn_b1", "L1_gnn_W2", "L1_gnn_b2"]


def kernel(**inputs):
    import numpy as np
    import concourse.bacc as bacc
    from concourse.bass_utils import run_bass_kernel_spmd

    nc = bacc.Bacc("TRN2", target_bir_lowering=False, num_devices=1)
    arrays = {f"in_{name}": np.ascontiguousarray(inputs[name]) for name in _INPUTS}
    args = [nc.dram_tensor(name, a.shape, mybir.dt.from_np(a.dtype), kind="ExternalInput").ap() for name, a in arrays.items()]
    out = nc.dram_tensor("out", (N, D), F32, kind="ExternalOutput").ap()
    x1_dram = nc.dram_tensor("x1_dram", (N, D), F32, kind="Internal").ap()
    gnn_program(nc, *args, out, x1_dram)
    return run_bass_kernel_spmd(nc, [arrays], core_ids=[0]).results[0]["out"]
```

```python
import math
from contextlib import ExitStack

import concourse.bass as bass
from concourse import mybir

F32 = mybir.dt.float32
F16 = mybir.dt.float16
BF16 = mybir.dt.bfloat16
U32 = mybir.dt.uint32
ALU = mybir.AluOpType
ACT = mybir.ActivationFunctionType
AX = mybir.AxisListType.X
ALL_MAX = bass.bass_isa.ReduceOp.max

P = 128
N, D, F = 4096, 512, 128
KD = D // P
NT = N // P
BANK = 512
XG = 4
IW = 256
IT = IW // P
NI = N // IW
NB = N // IW
NS = NI * NB
RING = 20
LAG = NB + 2
EXP_LAG = LAG - 1
STAGE = 3
ADJ_RING = 2
U_BANKS = 2 * IT
EPS = 1e-5

TOP = 2.0 ** 13
TINY = 2.0 ** -40
EXP_BITS = 0x7F800000
LOGIT = 0.5 / math.sqrt(D)
P_UP = 2.0 ** 12
X1_UP = 2.0 ** 10
Y_DOWN = 2.0 ** -18

X1_RING = 8
Y_FIRST = NS + 1
CW = 2 * IW
NC = N // CW
UNITS = NC * NB
UNIT = 2 * IT * IW
RAW_RING = 6
SLOTS = 33
Z_RING = 2
O_RING = 4
TW = CW // P
ORDER = [list(range(NC)), list(range(NC))[::-1]]
EARLY = 14
Y_LAST = (5, 9)
OUT_AT = 1
O_AT = (3, 6, 9, 12)


def unit_plan():
    units, loads, slot_of = [], [], {}
    free = [(0, slot) for slot in range(SLOTS)]
    for conv in range(2):
        for k, ic in enumerate(ORDER[conv]):
            for b in range(NB):
                n = len(units)
                load = None
                if conv == 0 or (ic, b) not in slot_of:
                    after, slot_of[ic, b] = free.pop(0)
                    load = len(loads)
                    loads.append((ic, b, slot_of[ic, b], after))
                units.append((conv, k, ic, b, load))
                if conv or n < UNITS - SLOTS:
                    free.append((n + 1, slot_of.pop((ic, b))))
    split_at = [[] for _ in units]
    for conv, first, end, start in ((0, EARLY, UNITS, 0), (1, UNITS, len(loads), 2)):
        for load in range(first, end):
            split_at[UNITS * conv + start + (load - first) * (UNITS - 1 - start) // (end - first)].append(load)
    own = {u[4]: n for n, u in enumerate(units)}
    for n, ls in enumerate(split_at):
        assert all(loads[l][3] <= n and own[l] >= n for l in ls)
    return units, loads, split_at


def gnn_program(nc, x, adj, wq, bq, wk, bk, wv, bv, w1, b1, w2, b2, out, x1_dram, g_dram, at_dram):
    with ExitStack() as ctx:
        def sb(name, shape, dt):
            return ctx.enter_context(nc.sbuf_tensor(name, shape, dt))

        def sem(name):
            return ctx.enter_context(nc.semaphore(name))

        xT = sb("xT", [P, 2, KD * N], F16)
        xv = sb("xv", [P, NT, D], F32)
        ring = sb("ring", [P, RING, BANK], F32)
        gT = sb("gT", [P, 2, 2 * KD * IW], F16)
        adj_in = sb("adj_in", [P, ADJ_RING, IT, 2 * IW], F32)
        stage = sb("stage", [P, STAGE, BANK], F32)
        pT = sb("pT", [P, 2, 2, BANK], F16)
        xr = sb("xr", [P, IT, D], F32)
        run_max = sb("run_max", [P, BANK], F32)
        den = sb("den", [P, BANK], F32)
        fold = sb("fold", [P, IW], F32)
        max_row = sb("max_row", [P, IW], F32)
        ident = sb("ident", [P, P], F32)
        ones = sb("ones", [P, P], F32)
        adj_max = sb("adj_max", [P, NB], F32)
        adj_all = sb("adj_all", [P, NI], F32)
        c_all = sb("c_all", [P, NT], F32)
        bq_c = sb("bq_c", [P, KD], F32)
        bk_c = sb("bk_c", [P, KD], F32)
        gb_c = sb("gb_c", [P, KD], F32)
        b1_c = sb("b1_c", [P, 1], F32)
        x_max = sb("x_max", [P, NT // XG], F32)
        q_max = sb("q_max", [P, IT], F32)
        bn = sb("bn", [P, 6], F32)
        mv = sb("mv", [P, IT, 2], F32)
        veps = sb("veps", [P, IT], F32)
        rstd = sb("rstd", [P, IT], F32)
        h_max = sb("h_max", [P, NC], F32)
        names = ["m0", "m1", "m2", "m3", "st_m", "st_wv", "st_w1", "st_gb", "mx_m", "mx_wv", "mx_w1", "mx_gb",
                 "e_m", "e_wv", "e_w1", "s_m", "s_wv", "s_w1", "mx_bv", "st_x", "mx_x", "e_x", "s_x", "k_g", "k_v",
                 "bound", "e_v", "s_v", "e_g", "s_g", "k_gs", "k_u", "k_l", "c0", "t0", "t1", "st_a", "mx_a",
                 "e_a", "s_a", "inv_h", "e_h", "s_h", "inv_z", "minus_half"]
        sc = sb("sc", [P, len(names)], F32)
        col = {name: sc[:, i:i + 1] for i, name in enumerate(names)}

        def cols(first, last):
            return sc[:, names.index(first):names.index(last) + 1]

        def flat(ap):
            return ap.rearrange("p a b -> p (a b)")

        def xt_block(part, k, tile, width=P):
            return xT[:, part, k * N + tile * P:k * N + tile * P + width]

        xt_tiles = [xT[:, part, :].rearrange("p (k n) -> p k n", k=KD) for part in range(2)]
        v_hl = xv[:, :, :].bitcast(F16).rearrange("p t (two d) -> p t two d", two=2)
        wq_raw, wk_raw, wv_raw = (ring[:, KD * i:KD * (i + 1), :] for i in range(3))
        wvT = flat(ring[:, 12:16, :]).bitcast(F16).rearrange("p (two k e) -> p two k e", two=2, k=KD)
        m_hl = flat(ring[:, 16:20, :]).bitcast(F16).rearrange("p (two k e) -> p two k e", two=2, k=KD)
        g_out = [flat(ring[:, 4 * i:4 * (i + 1), :]).bitcast(F16).rearrange("p (two k n) -> p two k n", two=2, k=KD)
                 for i in range(2)]
        p_flat = pT[:, :, :, :].rearrange("p a b c -> p (a b c)").bitcast(F32)
        c_row, bv_row = p_flat[:, 0:D], p_flat[:, D:2 * D]
        v_row = [xr[:, i, :] for i in range(2)]
        g_row = [stage[:, i, :] for i in range(2)]
        unused = stage[:, 2, :].bitcast(BF16)[:, 0:D]
        w1_stat = flat(adj_in[:, 0, :, :])[:, 0:KD * F]
        xt_f32 = flat(xT[:, :, :]).bitcast(F32)
        x1_in = [xt_f32[:, D * i:D * (i + 1)] for i in range(X1_RING)]
        hT = xt_f32[:, 0:N]
        y_hl = xt_f32[:, N:2 * N].bitcast(F16).rearrange("p (two t f) -> p two t f", two=2, t=NT)
        raw = [xt_f32[:, 2 * N + UNIT * i:2 * N + UNIT * (i + 1)] for i in range(RAW_RING)]
        rest = xt_f32[:, 2 * N + UNIT * RAW_RING:]
        w1_raw = rest[:, 0:KD * F]
        w1_hl = rest[:, D:2 * D].bitcast(F16).rearrange("p (two k f) -> p two k f", two=2, k=KD)
        x1T = [rest[:, D * (2 + i):D * (3 + i)].bitcast(F16).rearrange("p (two n) -> p two n", two=2) for i in range(2)]
        pairs = [ring[:, i % RING:i % RING + 2, :] for i in range(NS - RING, NS, 2)]
        split = [flat(gT[:, :, :])[:, 2 * UNIT * i:2 * UNIT * (i + 1)] for i in range(2)]
        split += [flat(adj_in[:, i, :, :]).bitcast(F16) for i in range(2)]
        split += [flat(pair).bitcast(F16) for pair in pairs]
        split += [flat(xv[:, 2 * i:2 * (i + 1), :]).bitcast(F16) for i in range(NT // 2)]
        split += [pT[:, :, :, :].rearrange("p a b c -> p (a b c)"), flat(stage[:, 0:2, :]).bitcast(F16),
                  flat(xr[:, :, :]).bitcast(F16)]
        split = [a.rearrange("p (two n) -> p two n", two=2) for a in split]
        assert len(split) == SLOTS
        h_hl = y_hl
        ht_place = [hT[:, D * i:D * (i + 1)] for i in range(8)]
        z_f, o_row, w2_s, b2_row = ht_place[0:2], ht_place[2:6], ht_place[6], ht_place[7]
        x1_res = [rest[:, D * i:D * (i + 1)] for i in range(O_RING)]

        bank = [ctx.enter_context(nc.psum_tensor(f"bank{i}", [P, BANK], F32)) for i in range(8)]
        s_bank, a_bank, misc, u_bank = bank[0:2], bank[2], bank[3], bank[4:8]
        m_bank = [bank[0], bank[1], bank[4], bank[5]]
        wvt_bank = [bank[7], bank[6], bank[2], bank[3]]
        xt_bank = [bank[2], bank[3]]
        acc_bank = bank[4:6]
        ht_bank = bank[0:3]
        o_bank = [bank[6], bank[7], bank[3]]

        d_small, d_wq, d_wk, d_wv, d_w1, d_late, d_x1 = (
            sem(s) for s in ("d_small", "d_wq", "d_wk", "d_wv", "d_w1", "d_late", "d_x1"))
        d_x = [sem(f"d_xgroup{i}") for i in range(NT // XG)]
        d_gout = [sem(f"d_gout{i}") for i in range(2)]
        d_gt = [sem(f"d_gt{i}") for i in range(2)]
        d_adj = [sem(f"d_adj{i}") for i in range(ADJ_RING)]
        d_at = [sem(f"d_at{i}") for i in range(STAGE)]
        d_xr = sem("d_xr")
        d_x1in = [sem(f"d_x1in{i}") for i in range(X1_RING)]
        d_raw = [sem(f"d_raw{i}") for i in range(RAW_RING)]
        d_res = [sem(f"d_res{i}") for i in range(O_RING)]
        d_out = [sem(f"d_out{i}") for i in range(O_RING)]
        p_pre, p_xt, p_v, p_g, p_at, p_qk, p_mt, p_mr, p_pv, p_den, p_x1t, p_y, p_unit, p_ht, p_o = (
            sem("p_" + s) for s in "pre xt v g at qk mt mr pv den x1t y unit ht o".split())
        a_pre, a_xt, a_v, a_gf, a_g, a_at, a_exp, a_p, a_mr, a_w1, a_x1t, a_y, a_unit, a_h, a_ht, a_z = (
            sem("a_" + s) for s in "pre xt v gf g at exp p mr w1 x1t y unit h ht z".split())
        v_st, v_sc, v_sx, v_pre, v_xt, v_c, v_vf, v_v, v_g, v_add, v_run, v_fold, v_diag, v_sub, v_p, v_abs = (
            sem("v_" + s) for s in "st sc sx pre xt c vf v g add run fold diag sub p abs".split())
        v_r, v_var, v_x1, v_w1, v_x1t, v_y, v_sa, v_scales, v_unit, v_h, v_ht, v_or, v_ovar, v_o, v_chain = (
            sem("v_" + s) for s in "r var x1 w1 x1t y sa scales unit h ht or ovar o chain".split())
        g_id, g_ar, g_den, g_rstd, g_res, g_orstd = (sem("g_" + s) for s in "id ar den rstd res orstd".split())

        units, loads, split_at = unit_plan()
        block = ctx.enter_context(nc.Block())

        @block.sync
        def _(sp):
            sp.dma_start(bq_c[:, :], bq.rearrange("(p k) -> p k", k=KD)).then_inc(d_small, 16)
            sp.dma_start(bk_c[:, :], bk.rearrange("(p k) -> p k", k=KD)).then_inc(d_small, 16)
            sp.dma_start(b1_c[:, :], b1.rearrange("(p o) -> p o", o=1)).then_inc(d_small, 16)
            sp.dma_start(wq_raw, wq.rearrange("(p k) d -> p k d", k=KD)).then_inc(d_wq, 16)
            sp.dma_start(wk_raw, wk.rearrange("(p k) d -> p k d", k=KD)).then_inc(d_wk, 16)
            sp.dma_start(bv_row, bv.rearrange("(o d) -> o d", o=1).broadcast_to([P, D])).then_inc(d_small, 16)
            sp.dma_start(w1_stat, w1.rearrange("(p k) f -> p (k f)", k=KD)).then_inc(d_small, 16)
            sp.dma_start(wv_raw, wv.rearrange("(k p) d -> p k d", p=P)).then_inc(d_wv, 16)
            x_tiles = x.rearrange("(t p) d -> p t d", p=P)
            for i in range(NT // XG):
                sp.dma_start(xv[:, XG * i:XG * (i + 1), :], x_tiles[:, XG * i:XG * (i + 1), :]).then_inc(d_x[i], 16)

            def load_adj(q):
                i, b = divmod(2 * q, NB)
                sp.dma_start(adj_in[:, q % ADJ_RING, :, :],
                             adj[IW * i:IW * (i + 1), IW * b:IW * (b + 2)].rearrange("(t p) c -> p t c", p=P)
                             ).then_inc(d_adj[q % ADJ_RING], 16)

            def load_gt(i):
                sp.dma_start(gT[:, i % 2, :], g_dram[i]).then_inc(d_gt[i % 2], 16)

            sp.wait_ge(v_st, 2)
            for q in range(ADJ_RING):
                load_adj(q)
            for g in range(NT // XG):
                sp.wait_ge(a_g, KD * (g + 1))
                sp.wait_ge(v_g, KD * (g + 1))
                for i in range(2):
                    sp.dma_start(g_dram[2 * g + i].rearrange("p (a n) -> p a n", n=IW),
                                 g_out[g % 2].rearrange("p a b n -> p (a b) n")[:, :, IW * i:IW * (i + 1)]
                                 ).then_inc(d_gout[g % 2], 16)
                if g == 1:
                    sp.wait_ge(d_gout[0], 32)
                    load_gt(0)
                    load_gt(1)
            sp.wait_ge(v_vf, NT)
            sp.wait_ge(a_v, NT)
            sp.wait_ge(v_v, NT)
            x_chunks = x.rearrange("(i t p) d -> i p t d", t=IT, p=P)
            x1_chunks = x1_dram.rearrange("(i t p) d -> i p t d", t=IT, p=P)
            sp.dma_start(xr[:, :, :], x_chunks[0]).then_inc(d_xr, 16)
            for g in range(2):
                sp.wait_ge(d_gout[g], 32 * (NT // XG // 2))

            def load_raw(l):
                ic, b = loads[l][:2]
                if l >= RAW_RING:
                    sp.wait_ge(a_unit, l - RAW_RING + 1)
                    sp.wait_ge(v_unit, l - RAW_RING + 1)
                sp.dma_start(raw[l % RAW_RING].rearrange("p (i c) -> p i c", i=2),
                             at_dram.rearrange("(c i b) p n -> c b p i n", i=2, b=NB)[ic, b]
                             ).then_inc(d_raw[l % RAW_RING], 16)

            def load_x1(t):
                if t >= X1_RING:
                    sp.wait_ge(p_x1t, t - X1_RING + 1)
                sp.dma_start(x1_in[t % X1_RING], x1_dram[P * t:P * (t + 1), :]).then_inc(d_x1in[t % X1_RING], 16)

            x1_loads = 0
            for s in range(NS + LAG + 4):
                if s < NS:
                    sp.wait_ge(a_at, s + 1)
                    sp.dma_start(at_dram[s], stage[:, s % STAGE, :]).then_inc(d_at[s % STAGE], 16)
                    if s % 2 and s // 2 + ADJ_RING < NS // 2:
                        sp.wait_ge(p_at, s + 1)
                        load_adj(s // 2 + ADJ_RING)
                    i, b = divmod(s, NB)
                    if b == 0 and 1 <= i < NI - 1:
                        sp.wait_ge(p_qk, s)
                        load_gt(i + 1)
                j, b = divmod(s, NB)
                if b == 5 and 2 <= j < NI + 1:
                    sp.wait_ge(v_x1, j - 1)
                    sp.dma_start(x1_chunks[j - 2], xr[:, :, :]).then_inc(d_x1, 16)
                if b == 7 and 2 <= j < NI + 1:
                    sp.wait_ge(d_x1, 16 * (j - 1))
                    sp.dma_start(xr[:, :, :], x_chunks[j - 1]).then_inc(d_xr, 16)
                if s == NS:
                    sp.wait_ge(p_qk, NS)
                    sp.dma_start(w1_raw, w1.rearrange("(k p) f -> p k f", p=P)).then_inc(d_w1, 16)
                    for t in range(X1_RING):
                        load_x1(t)
                    x1_loads = X1_RING
                    for i in range(STAGE):
                        sp.wait_ge(d_at[i], 16 * len(range(i, NS, STAGE)))
                    for l in range(RAW_RING):
                        load_raw(l)
                if NS + LAG - EARLY <= s < NS + LAG:
                    load_raw(RAW_RING + s - (NS + LAG - EARLY))
                if s > Y_FIRST:
                    for _ in range(2):
                        if x1_loads < NT - 2 and (x1_loads < NT - 4 or s >= NS + 7):
                            load_x1(x1_loads)
                            x1_loads += 1
            sp.wait_ge(v_x1, NI)
            sp.dma_start(x1_chunks[NI - 1], xr[:, :, :]).then_inc(d_x1, 16)
            for l in range(RAW_RING + EARLY, len(loads)):
                if l == UNITS + RAW_RING + NC:
                    sp.wait_ge(p_ht, NC)
                    sp.dma_start(w2_s, w2[:, :]).then_inc(d_late, 16)
                    sp.dma_start(b2_row, b2.rearrange("(o d) -> o d", o=1).broadcast_to([P, D])).then_inc(d_late, 16)
                load_raw(l)

        @block.tensor
        def _(pe):
            def product(dst, pairs):
                for i, (ah, al, bh, bl) in enumerate(pairs):
                    pe.matmul(dst, ah, bh, start=(i == 0), stop=False)
                    pe.matmul(dst, ah, bl, start=False, stop=False)
                    last = pe.matmul(dst, al, bh, start=False, stop=(i == len(pairs) - 1))
                return last

            def accumulate(dst, pairs):
                for i, (a, b) in enumerate(pairs):
                    last = pe.matmul(dst, a, b, start=(i == 0), stop=(i == len(pairs) - 1))
                return last

            pe.wait_ge(d_wq, 16)
            pe.wait_ge(d_wk, 16)
            for k in range(KD):
                accumulate(m_bank[k][:, :], [(wq_raw[:, e, P * k:P * (k + 1)], wk_raw[:, e, :]) for e in range(KD)]
                           ).then_inc(p_pre, 1)
            pe.wait_ge(d_small, 16 * 5)
            for k in range(KD):
                last = accumulate(bank[2][:, k:k + 1], [(wk_raw[:, e, P * k:P * (k + 1)], bq_c[:, e:e + 1]) for e in range(KD)])
            last.then_inc(p_pre, 1)
            everywhere = [P, P]
            accumulate(bank[3][:, :], [(bk_c[:, e:e + 1].broadcast_to(everywhere), wq_raw[:, e, :]) for e in range(KD)]
                       ).then_inc(p_pre, 1)
            accumulate(bank[6][:, 0:1], [(bq_c[:, e:e + 1].broadcast_to(everywhere), bk_c[:, e:e + 1]) for e in range(KD)]
                       ).then_inc(p_pre, 1)
            pe.wait_ge(g_id, 2)
            pe.wait_ge(d_wv, 16)
            for k in range(KD):
                if k == 1:
                    pe.wait_ge(v_pre, 3)
                for e in range(KD):
                    last = pe.transpose(wvt_bank[k][:, P * e:P * (e + 1)], wv_raw[:, e, P * k:P * (k + 1)], ident[:, :])
                last.then_inc(p_pre, 1)
            pe.wait_ge(a_pre, 2 * KD)
            pe.wait_ge(v_pre, 3 + 2 * KD)

            def x_transpose(t):
                pe.wait_ge(d_x[t // XG], 16)
                if t >= 2:
                    pe.wait_ge(a_xt, t - 1)
                    pe.wait_ge(v_xt, t - 1)
                for k in range(KD):
                    last = pe.transpose(xt_bank[t % 2][:, P * k:P * (k + 1)], xv[:, t, P * k:P * (k + 1)], ident[:, :])
                last.then_inc(p_xt, 1)

            x_transpose(0)
            for t in range(NT):
                if t + 1 < NT:
                    x_transpose(t + 1)
                pe.wait_ge(a_xt, t + 1)
                pe.wait_ge(v_xt, t + 1)
                if t >= U_BANKS:
                    pe.wait_ge(v_vf, t - U_BANKS + 1)
                product(u_bank[t % U_BANKS][:, :],
                        [(xt_block(0, k, t), xt_block(1, k, t), wvT[:, 0, k, :], wvT[:, 1, k, :]) for k in range(KD)]
                        ).then_inc(p_v, 1)
                if t % XG == XG - 1:
                    first = t - XG + 1
                    for kk in range(KD):
                        n = KD * (t // XG) + kk
                        if n >= 2:
                            pe.wait_ge(a_gf, n - 1)
                        product(s_bank[n % 2][:, :],
                                [(m_hl[:, 0, k, P * kk:P * (kk + 1)], m_hl[:, 1, k, P * kk:P * (kk + 1)],
                                  xt_block(0, k, first, BANK), xt_block(1, k, first, BANK)) for k in range(KD)]
                                ).then_inc(p_g, 1)
            pe.wait_ge(a_gf, NT // XG * KD)
            pe.wait_ge(v_vf, NT)

            def adj_transpose(s):
                q = s // 2
                pe.wait_ge(d_adj[q % ADJ_RING], 16 * (q // ADJ_RING + 1))
                if s >= 1:
                    pe.wait_ge(a_at, s)
                for jj in range(IT):
                    for t in range(IT):
                        c = IW * (s % 2) + P * jj
                        last = pe.transpose(a_bank[:, IW * jj + P * t:IW * jj + P * (t + 1)],
                                            adj_in[:, q % ADJ_RING, t, c:c + P], ident[:, :])
                last.then_inc(p_at, 1)

            def logits(s):
                i, b = divmod(s, NB)
                if b == 0:
                    pe.wait_ge(d_gt[i % 2], 16 * (i // 2 + 1))
                if s >= 2:
                    pe.wait_ge(v_add, s - 1)
                g = gT[:, i % 2, :].rearrange("p (two k n) -> p two k n", two=2, k=KD)
                for jj in range(IT):
                    last = product(s_bank[s % 2][:, IW * jj:IW * (jj + 1)],
                                   [(xt_block(0, k, IT * b + jj), xt_block(1, k, IT * b + jj), g[:, 0, k, :], g[:, 1, k, :])
                                    for k in range(KD)])
                last.then_inc(p_qk, 1)

            def max_transpose(i):
                pe.wait_ge(v_fold, i + 1)
                if i >= 2:
                    pe.wait_ge(v_r, IT * (i - 1))
                for t in range(IT):
                    last = pe.transpose(misc[:, P * t:P * (t + 1)], fold[:, P * t:P * (t + 1)], ident[:, :])
                last.then_inc(p_mt, 1)

            def max_to_row(i):
                pe.wait_ge(v_diag, i + 1)
                pe.matmul(misc[:, 0:IW], ones[:, :], fold[:, :], start=True, stop=True).then_inc(p_mr, 1)

            def attend(s):
                i, b = divmod(s, NB)
                pe.wait_ge(a_p, s + 1)
                pe.wait_ge(v_p, s + 1)
                if s == 0:
                    pe.wait_ge(a_v, NT)
                    pe.wait_ge(v_v, NT)
                if b == 0 and i >= 2:
                    pe.wait_ge(v_r, IT * (i - 1))
                for t in range(IT):
                    dst = u_bank[IT * (i % 2) + t][:, :]
                    for jj in range(IT):
                        c = IW * jj + P * t
                        ah, al = pT[:, s % 2, 0, c:c + P], pT[:, s % 2, 1, c:c + P]
                        vh, vl = v_hl[:, IT * b + jj, 0, :], v_hl[:, IT * b + jj, 1, :]
                        end = b == NB - 1 and jj == IT - 1
                        pe.matmul(dst, ah, vh, start=(b == 0 and jj == 0), stop=False)
                        pe.matmul(dst, ah, vl, start=False, stop=False)
                        last = pe.matmul(dst, al, vh, start=False, stop=end)
                last.then_inc(p_pv, 1)

            def denominators(i):
                pe.wait_ge(g_den, NB * (i + 1))
                pe.wait_ge(a_mr, min(i + 2, NI))
                for t in range(IT):
                    last = accumulate(misc[:, t:t + 1], [(den[:, IW * jj + P * t:IW * jj + P * (t + 1)], ones[:, 0:1])
                                                         for jj in range(IT)])
                last.then_inc(p_den, 1)

            def x1_transpose(t):
                if t < NT - IT:
                    pe.wait_ge(d_x1in[t % X1_RING], 16 * (t // X1_RING + 1))
                    src = x1_in[t % X1_RING]
                else:
                    pe.wait_ge(v_x1, NI)
                    src = xr[:, t - (NT - IT), :]
                if t >= 2:
                    pe.wait_ge(a_x1t, t - 1)
                    pe.wait_ge(v_x1t, t - 1)
                for k in range(KD):
                    last = pe.transpose(bank[t % 2][:, P * k:P * (k + 1)], src[:, P * k:P * (k + 1)], ident[:, :])
                last.then_inc(p_x1t, 1)

            def y_rows(n):
                pe.wait_ge(a_x1t, 2 * n + 2)
                pe.wait_ge(v_x1t, 2 * n + 2)
                pe.wait_ge(a_w1, 1)
                pe.wait_ge(v_w1, 1)
                if n >= 1:
                    pe.wait_ge(a_y, n)
                    pe.wait_ge(v_y, n)
                for i in range(2):
                    last = product(a_bank[:, F * i:F * (i + 1)],
                                   [(x1T[i][:, 0, P * k:P * (k + 1)], x1T[i][:, 1, P * k:P * (k + 1)],
                                     w1_hl[:, 0, k, :], w1_hl[:, 1, k, :]) for k in range(KD)])
                last.then_inc(p_y, 1)

            for s in range(NS + LAG):
                j, b = divmod(s, NB)
                if s < NS:
                    adj_transpose(s)
                    logits(s)
                if b == 0 and 1 <= j <= NI:
                    max_transpose(j - 1)
                y = s - Y_FIRST
                if 0 < y < NT // 2:
                    y_rows(y - 1)
                if 0 <= y < NT // 2 - 1:
                    if y == 0:
                        pe.wait_ge(v_add, NS)
                        pe.wait_ge(a_at, NS)
                    x1_transpose(2 * y)
                    x1_transpose(2 * y + 1)
                if s >= LAG:
                    attend(s - LAG)
                if b == 0 and 1 <= j <= NI:
                    max_to_row(j - 1)
                if b == 1 and j >= 2:
                    denominators(j - 2)

            def h_transpose(g):
                pe.wait_ge(v_h, g + 1)
                if g >= 3:
                    pe.wait_ge(a_ht, g - 2)
                    pe.wait_ge(v_ht, g - 2)
                for i in range(TW):
                    last = pe.transpose(ht_bank[g % 3][:, P * i:P * (i + 1)],
                                        hT[:, CW * g + P * i:CW * g + P * (i + 1)], ident[:, :])
                last.then_inc(p_ht, 1)

            def o_rows(n):
                k, i = divmod(n, TW)
                if i == 0:
                    pe.wait_ge(a_z, k + 1)
                if n >= 3:
                    pe.wait_ge(v_or, n - 2)
                pe.matmul(o_bank[n % 3][:, :], z_f[k % Z_RING][:, P * i:P * (i + 1)], w2_s, start=True, stop=True).then_inc(p_o, 1)

            pe.wait_ge(a_y, NT // 2 - 1)
            pe.wait_ge(v_y, NT // 2 - 1)
            pe.wait_ge(v_r, NT - IT)
            unit_split = {(ic, b): split[slot] for ic, b, slot, _ in loads[:UNITS]}
            for conv, k, ic, b, load in units:
                if load is not None:
                    pe.wait_ge(a_unit, load + 1)
                    pe.wait_ge(v_unit, load + 1)
                    unit_split[ic, b] = split[loads[load][2]]
                n = NC * conv + k
                if n == 0:
                    if b == Y_LAST[0]:
                        x1_transpose(NT - 2)
                        x1_transpose(NT - 1)
                    if b == Y_LAST[1]:
                        y_rows(NT // 2 - 1)
                    if b == NB - 1:
                        pe.wait_ge(a_y, NT // 2)
                        pe.wait_ge(v_y, NT // 2)
                if b == 0 and 2 <= n <= NC + 1:
                    pe.wait_ge(a_h, n - 1)
                if b == 0 and n > NC + 1:
                    pe.wait_ge(a_z, n - NC - 1)
                if conv == 1 and k == 0 and b == 0:
                    for g in range(3):
                        h_transpose(g)
                if conv == 1 and k == 0 and b % 2 == 0:
                    if b // 2 + 3 < NC:
                        h_transpose(b // 2 + 3)
                    pe.wait_ge(a_ht, b // 2 + 1)
                    pe.wait_ge(v_ht, b // 2 + 1)
                dst = acc_bank[n % 2][:, :].rearrange("p (i c) -> p i c", i=2)
                rhs = [unit_split[ic, b][:, part, :].rearrange("p (i j c) -> p i j c", i=2, j=IT) for part in range(2)]
                lhs = (y_hl, h_hl)[conv]
                for jj in range(IT):
                    wh, wl = lhs[:, 0, IT * b + jj, :], lhs[:, 1, IT * b + jj, :]
                    rh, rl = rhs[0][:, :, jj, :], rhs[1][:, :, jj, :]
                    pe.matmul(dst, wh, rh, start=(b == 0 and jj == 0), stop=False)
                    pe.matmul(dst, wh, rl, start=False, stop=False)
                    last = pe.matmul(dst, wl, rh, start=False, stop=(b == NB - 1 and jj == IT - 1))
                last.then_inc(p_unit, 1)
                if conv == 1 and k >= 1 and b in O_AT:
                    if k == 1 and b == O_AT[0]:
                        pe.wait_ge(d_late, 32)
                        pe.wait_ge(v_r, NT)
                    o_rows(TW * (k - 1) + O_AT.index(b))
            for n in range(NT - TW, NT):
                o_rows(n)

        @block.scalar
        def _(act):
            act.wait_ge(v_sc, 1)
            for k in range(KD):
                act.wait_ge(p_pre, 1 + k)
                act.activation(m_hl[:, 0, k, :], m_bank[k][:, :], ACT.Identity, scale=col["s_m"]).then_inc(a_pre, 1)
            for k in range(KD):
                act.wait_ge(p_pre, 8 + k)
                act.activation(wvT[:, 0, k, :], wvt_bank[k][:, :], ACT.Identity, scale=col["s_wv"]).then_inc(a_pre, 1)

            def xt_hi(t):
                act.wait_ge(p_xt, t + 1)
                act.activation(xt_tiles[0][:, :, P * t:P * (t + 1)], xt_bank[t % 2][:, :].rearrange("p (k n) -> p k n", k=KD),
                               ACT.Identity, scale=col["s_x"]).then_inc(a_xt, 1)

            def g_hi(n):
                g, kk = divmod(n, KD)
                act.wait_ge(p_g, n + 1)
                if n >= 2:
                    act.wait_ge(v_g, n - 1)
                act.activation(g_row[n % 2], s_bank[n % 2][:, :], ACT.Identity, bias=gb_c[:, kk:kk + 1],
                               scale=col["k_gs"]).then_inc(a_gf, 1)
                if g >= 2 and kk == 0:
                    act.wait_ge(d_gout[g % 2], 32 * (g // 2))
                if n == 0:
                    act.wait_ge(p_pre, 11)
                act.wait_ge(a_gf, n + 1)
                act.activation(g_out[g % 2][:, 0, kk, :], g_row[n % 2], ACT.Copy).then_inc(a_g, 1)

            act.wait_ge(v_sx, 1)
            xt_hi(0)
            act.wait_ge(v_scales, 1)
            for t in range(NT):
                if t + 1 < NT:
                    xt_hi(t + 1)
                if t % XG == 0 and t > 0:
                    g_hi(KD * (t // XG) - 1)
                act.wait_ge(v_vf, t + 1)
                act.wait_ge(v_c, t + 1)
                act.activation(v_hl[:, t, 0, :], v_row[t % 2], ACT.Identity, scale=col["s_v"]).then_inc(a_v, 1)
                if t % XG == XG - 1:
                    for kk in range(KD - 1):
                        g_hi(KD * (t // XG) + kk)
            g_hi(NT // XG * KD - 1)

            def x1_hi(t):
                act.wait_ge(p_x1t, t + 1)
                if t >= 2:
                    act.wait_ge(p_y, t // 2)
                act.activation(x1T[t % 2][:, 0, :], bank[t % 2][:, :], ACT.Copy, scale=X1_UP).then_inc(a_x1t, 1)

            def y_hi(n):
                act.wait_ge(p_y, n + 1)
                act.activation(y_hl[:, 0, 2 * n:2 * n + 2, :], a_bank[:, 0:2 * F].rearrange("p (t f) -> p t f", f=F),
                               ACT.Copy, scale=Y_DOWN).then_inc(a_y, 1)

            def h_out(n):
                act.wait_ge(p_unit, NB * (n + 1))
                act.activation(hT[:, CW * n:CW * (n + 1)], acc_bank[n % 2][:, :], ACT.Relu, bias=b1_c[:, :],
                               scale=col["inv_h"]).then_inc(a_h, 1)

            def z_out(n):
                act.wait_ge(p_unit, NB * (NC + n + 1))
                if n >= Z_RING:
                    act.wait_ge(p_o, TW * (n - Z_RING + 1))
                act.activation(z_f[n % Z_RING], acc_bank[n % 2][:, :], ACT.Copy, scale=col["inv_z"]).then_inc(a_z, 1)

            def unit_hi(load):
                _, _, slot, after = loads[load]
                if load == 0:
                    act.wait_ge(v_sa, 1)
                act.wait_ge(d_raw[load % RAW_RING], 16 * (load // RAW_RING + 1))
                if 4 <= load < 4 + RING // 2:
                    last = NS - RING + 2 * (load - 4) + 2
                    act.wait_ge(v_p, last)
                    act.wait_ge(g_den, last)
                elif load == 4 + RING // 2:
                    act.wait_ge(p_pv, NS)
                elif load == SLOTS - 1:
                    act.wait_ge(p_x1t, NT)
                    act.wait_ge(d_x1, 16 * NI)
                elif after:
                    act.wait_ge(p_unit, after)
                act.activation(split[slot][:, 0, :], raw[load % RAW_RING], ACT.Copy, scale=col["s_a"]).then_inc(a_unit, 1)

            for s in range(NS + LAG):
                if s < NS:
                    act.wait_ge(p_at, s + 1)
                    if s >= STAGE:
                        act.wait_ge(d_at[s % STAGE], 16 * (s // STAGE))
                        act.wait_ge(v_abs, s - STAGE + 1)
                    elif s == 0:
                        act.wait_ge(v_g, NT // XG * KD)
                        act.wait_ge(v_c, NT)
                    act.activation(stage[:, s % STAGE, :], a_bank[:, :], ACT.Copy).then_inc(a_at, 1)
                e = s - EXP_LAG
                if 0 <= e < NS:
                    act.wait_ge(v_sub, e + 1)
                    p = ring[:, e % RING, :]
                    act.activation(p, p, ACT.Exp, scale=2.0).then_inc(a_exp, 1)
                    if e >= 2:
                        act.wait_ge(p_pv, e - 1)
                    act.wait_ge(a_exp, e + 1)
                    act.activation(pT[:, e % 2, 0, :], p, ACT.Copy, scale=P_UP).then_inc(a_p, 1)
                j, b = divmod(s, NB)
                if b == 0 and 1 <= j <= NI:
                    act.wait_ge(p_mr, j)
                    if j >= 2:
                        act.wait_ge(v_sub, NB * (j - 1))
                    act.activation(max_row[:, :], misc[:, 0:IW], ACT.Copy).then_inc(a_mr, 1)
                if s == NS:
                    act.wait_ge(d_w1, 16)
                    act.activation(w1_hl[:, 0, :, :].rearrange("p k f -> p (k f)"), w1_raw, ACT.Identity,
                                   scale=col["s_w1"]).then_inc(a_w1, 1)
                y = s - Y_FIRST
                if 0 < y < NT // 2:
                    y_hi(y - 1)
                if 0 <= y < NT // 2 - 1:
                    x1_hi(2 * y)
                    x1_hi(2 * y + 1)
                if s >= NS + LAG - EARLY:
                    unit_hi(s - (NS + LAG - EARLY))

            for n, (conv, k, ic, b, _) in enumerate(units):
                for load in split_at[n]:
                    unit_hi(load)
                if conv == k == 0 and b == Y_LAST[0]:
                    x1_hi(NT - 2)
                    x1_hi(NT - 1)
                if conv == k == 0 and b == Y_LAST[1]:
                    y_hi(NT // 2 - 1)
                if conv == 1 and k == 0 and b == 0:
                    h_out(NC - 1)
                    for g in range(NC):
                        act.wait_ge(p_ht, g + 1)
                        act.activation(h_hl[:, 0, TW * g:TW * (g + 1), :], ht_bank[g % 3][:, :].rearrange("p (t f) -> p t f", f=F),
                                       ACT.Copy).then_inc(a_ht, 1)
                elif b == OUT_AT and k >= 1:
                    (h_out, z_out)[conv](k - 1)
            z_out(NC - 1)

        @block.vector
        def _(dve):
            chained = [0]

            def link(ins):
                chained[0] += 1
                ins.then_inc(v_chain, 1)
                dve.wait_ge(v_chain, chained[0])

            def abs_max(dst, src):
                return dve.tensor_reduce(dst, src, AX, ALU.max, apply_absolute_value=True)

            def power(dst, src):
                link(dve.tensor_scalar(dst, src, TINY, None, ALU.max))
                link(dve.tensor_scalar(dst.bitcast(U32), dst.bitcast(U32), EXP_BITS, None, ALU.bitwise_and))

            def scale_of(dst, power_of):
                link(dve.reciprocal(dst, power_of))
                link(dve.tensor_scalar(dst, dst, TOP, None, ALU.mult))

            def minus_hi(dst, src, scale, hi):
                return dve.scalar_tensor_tensor(dst, src, scale, hi, ALU.mult, ALU.subtract)

            def group_max(i):
                dve.wait_ge(d_x[i], 16)
                link(abs_max(x_max[:, i:i + 1], flat(xv[:, XG * i:XG * (i + 1), :])))

            dve.wait_ge(d_small, 16 * 5)
            abs_max(col["mx_bv"], bv_row).then_inc(v_st, 1)
            abs_max(col["st_w1"], w1_stat).then_inc(v_st, 1)
            dve.wait_ge(d_wv, 16)
            abs_max(col["st_wv"], flat(wv_raw)).then_inc(v_st, 1)
            for i in range(3):
                group_max(i)
            for k in range(KD):
                dve.wait_ge(p_pre, 1 + k)
                link(abs_max(col[f"m{k}"], m_bank[k][:, :]))
            dve.tensor_reduce(col["st_m"], cols("m0", "m3"), AX, ALU.max).then_inc(v_st, 1)
            group_max(3)
            dve.wait_ge(p_pre, 7)
            link(dve.tensor_scalar(gb_c[:, :], bank[2][:, 0:KD], LOGIT, None, ALU.mult))
            abs_max(col["st_gb"], gb_c[:, :]).then_inc(v_st, 1)
            dve.tensor_copy(c_row, bank[3][:, :]).then_inc(v_pre, 2)
            dve.tensor_copy(col["c0"], bank[6][:, 0:1]).then_inc(v_pre, 1)
            group_max(4)
            dve.wait_ge(g_ar, 1)
            power(cols("e_m", "e_w1"), cols("mx_m", "mx_w1"))
            link(dve.reciprocal(cols("s_m", "s_w1"), cols("e_m", "e_w1")))
            dve.tensor_scalar(cols("s_m", "s_w1"), cols("s_m", "s_w1"), TOP, None, ALU.mult).then_inc(v_sc, 1)
            dve.wait_ge(v_sc, 1)
            group_max(5)
            for k in range(KD):
                dve.wait_ge(a_pre, 1 + k)
                minus_hi(m_hl[:, 1, k, :], m_bank[k][:, :], col["s_m"], m_hl[:, 0, k, :]).then_inc(v_pre, 1)
            group_max(6)
            for k in range(KD):
                dve.wait_ge(a_pre, 1 + KD + k)
                minus_hi(wvT[:, 1, k, :], wvt_bank[k][:, :], col["s_wv"], wvT[:, 0, k, :]).then_inc(v_pre, 1)
            group_max(7)
            dve.tensor_reduce(col["st_x"], x_max[:, :], AX, ALU.max).then_inc(v_st, 1)
            dve.wait_ge(g_ar, 2)
            power(col["e_x"], col["mx_x"])
            link(dve.reciprocal(col["s_x"], col["e_x"]))
            dve.tensor_scalar(col["s_x"], col["s_x"], TOP, None, ALU.mult).then_inc(v_sx, 1)
            dve.wait_ge(v_sx, 1)
            link(dve.tensor_scalar(col["k_g"], col["e_x"], col["e_m"], LOGIT / TOP ** 2, ALU.mult, ALU.mult))
            link(dve.tensor_scalar(col["k_v"], col["e_x"], col["e_wv"], 1 / TOP ** 2, ALU.mult, ALU.mult))
            link(dve.tensor_scalar(col["bound"], col["k_g"], 4.0 * D * TOP ** 2, col["mx_gb"], ALU.mult, ALU.add))
            power(col["e_g"], col["bound"])
            scale_of(col["s_g"], col["e_g"])
            link(dve.tensor_tensor(col["k_gs"], col["k_g"], col["s_g"], ALU.mult))
            link(dve.tensor_scalar(gb_c[:, :], gb_c[:, :], col["s_g"], None, ALU.mult))
            link(dve.tensor_scalar(col["k_l"], col["e_x"], col["e_g"], 1 / TOP ** 2, ALU.mult, ALU.mult))
            link(dve.tensor_scalar(col["bound"], col["k_v"], 4.0 * D * TOP ** 2, col["mx_bv"], ALU.mult, ALU.add))
            power(col["e_v"], col["bound"])
            scale_of(col["s_v"], col["e_v"])
            dve.tensor_scalar(col["k_u"], col["e_v"], 1 / (TOP * P_UP), None, ALU.mult).then_inc(v_scales, 1)
            dve.wait_ge(v_scales, 1)

            def xt_lo(t):
                dve.wait_ge(a_xt, t + 1)
                minus_hi(xt_tiles[1][:, :, P * t:P * (t + 1)], xt_bank[t % 2][:, :].rearrange("p (k n) -> p k n", k=KD),
                         col["s_x"], xt_tiles[0][:, :, P * t:P * (t + 1)]).then_inc(v_xt, 1)

            def g_lo(n):
                dve.wait_ge(a_g, n + 1)
                hi, lo = (g_out[n // KD % 2][:, part, n % KD, :] for part in range(2))
                dve.tensor_tensor(lo, g_row[n % 2], hi, ALU.subtract).then_inc(v_g, 1)

            xt_lo(0)
            for t in range(NT):
                if t + 1 < NT:
                    xt_lo(t + 1)
                if t % XG == 0 and t > 0:
                    g_lo(KD * (t // XG) - 1)
                dve.tensor_tensor_reduce(unused, xv[:, t, :], c_row, 1.0, 0.0, ALU.mult, ALU.add, col["t0"]).then_inc(v_c, 1)
                dve.wait_ge(v_c, t + 1)
                link(dve.tensor_scalar(c_all[:, t:t + 1], col["t0"], col["c0"], LOGIT, ALU.add, ALU.mult))
                dve.wait_ge(p_v, t + 1)
                if t >= 2:
                    dve.wait_ge(a_v, t - 1)
                dve.scalar_tensor_tensor(v_row[t % 2], u_bank[t % U_BANKS][:, :], col["k_v"], bv_row,
                                         ALU.mult, ALU.add).then_inc(v_vf, 1)
                dve.wait_ge(a_v, t + 1)
                dve.wait_ge(v_vf, t + 1)
                minus_hi(v_hl[:, t, 1, :], v_row[t % 2], col["s_v"], v_hl[:, t, 0, :]).then_inc(v_v, 1)
                if t % XG == XG - 1:
                    for kk in range(KD - 1):
                        g_lo(KD * (t // XG) + kk)
            g_lo(NT // XG * KD - 1)

            def halves(ap):
                return ap.rearrange("p (j i) -> p j i", j=IT)

            def subtract_max(e):
                if e % NB == 0:
                    dve.wait_ge(a_mr, e // NB + 1)
                    dve.wait_ge(v_run, e + NB)
                p = ring[:, e % RING, :]
                dve.tensor_tensor(halves(p), halves(p), max_row[:, :].unsqueeze(1).broadcast_to([P, IT, IW]),
                                  ALU.subtract).then_inc(v_sub, 1)

            def add_adj(s):
                dve.wait_ge(p_qk, s + 1)
                dve.wait_ge(a_at, s + 1)
                if s >= RING:
                    dve.wait_ge(a_p, s - RING + 1)
                    dve.wait_ge(v_p, s - RING + 1)
                    dve.wait_ge(g_den, s - RING + 1)
                elif s == 0:
                    for i in range(2):
                        dve.wait_ge(d_gout[i], 32 * (NT // XG // 2))
                dve.scalar_tensor_tensor(ring[:, s % RING, :], s_bank[s % 2][:, :], col["k_l"], stage[:, s % STAGE, :],
                                         ALU.mult, ALU.add).then_inc(v_add, 1)

            def running_max(s):
                dve.wait_ge(v_add, s + 1)
                b = s % NB
                if b >= 2:
                    dve.wait_ge(v_run, s)
                if b == 0:
                    return
                before = ring[:, (s - 1) % RING, :] if b == 1 else run_max[:, :]
                dve.tensor_tensor(run_max[:, :], before, ring[:, s % RING, :], ALU.max).then_inc(v_run, 1 + (b == 1))

            def fold_max(i):
                dve.wait_ge(v_run, NB * (i + 1))
                if i >= 1:
                    dve.wait_ge(p_mr, i)
                dve.tensor_tensor(fold[:, :], run_max[:, 0:IW], run_max[:, IW:2 * IW], ALU.max).then_inc(v_fold, 1)

            def max_diagonals(i):
                dve.wait_ge(p_mt, i + 1)
                link(dve.tensor_reduce(q_max[:, :], misc[:, 0:IW].rearrange("p (t n) -> p t n", t=IT), AX, ALU.max))
                c = c_all[:, IT * i:IT * (i + 1)]
                link(dve.tensor_tensor(q_max[:, :], q_max[:, :], c, ALU.add))
                link(dve.tensor_tensor(q_max[:, :], q_max[:, :], c, ALU.subtract))
                for t in range(IT):
                    last = dve.tensor_scalar(fold[:, P * t:P * (t + 1)], ident[:, :], q_max[:, t:t + 1], None, ALU.mult)
                    if t < IT - 1:
                        link(last)
                last.then_inc(v_diag, 1)

            def p_lo(e):
                dve.wait_ge(a_p, e + 1)
                minus_hi(pT[:, e % 2, 1, :], ring[:, e % RING, :], P_UP, pT[:, e % 2, 0, :]).then_inc(v_p, 1)

            def adj_maximum(s):
                i, b = divmod(s, NB)
                abs_max(adj_max[:, b:b + 1], stage[:, s % STAGE, :]).then_inc(v_abs, 1)
                if b == NB - 1:
                    dve.wait_ge(v_abs, s + 1)
                    link(dve.tensor_reduce(adj_all[:, i:i + 1], adj_max[:, :], AX, ALU.max))

            def attention_rows(i, t):
                r = xr[:, t, :]
                if t == 0:
                    dve.wait_ge(p_pv, NB * (i + 1))
                    dve.wait_ge(p_den, i + 1)
                    dve.wait_ge(d_xr, 16 * (i + 1))
                link(dve.reciprocal(col["t0"], misc[:, t:t + 1]))
                link(dve.tensor_scalar(col["t1"], col["t0"], col["k_u"], None, ALU.mult))
                dve.scalar_tensor_tensor(r, u_bank[IT * (i % 2) + t][:, :], col["t1"], r, ALU.mult, ALU.add).then_inc(v_r, 1)
                dve.wait_ge(v_r, IT * i + t + 1)
                link(dve.bn_stats(bn[:, :], r))
                link(dve.bn_aggr(mv[:, t, :], bn[:, :]))
                ins = dve.tensor_scalar(veps[:, t:t + 1], mv[:, t, 1:2], EPS, None, ALU.add)
                if t == IT - 1:
                    ins.then_inc(v_var, 1)

            def normalise(i):
                dve.wait_ge(g_rstd, i + 1)
                for t in range(IT):
                    ins = dve.tensor_scalar(xr[:, t, :], xr[:, t, :], mv[:, t, 0:1], rstd[:, t:t + 1], ALU.subtract, ALU.mult)
                ins.then_inc(v_x1, 1)

            def x1_lo(t):
                dve.wait_ge(a_x1t, t + 1)
                minus_hi(x1T[t % 2][:, 1, :], bank[t % 2][:, :], X1_UP, x1T[t % 2][:, 0, :]).then_inc(v_x1t, 1)

            def y_lo(n):
                dve.wait_ge(a_y, n + 1)
                minus_hi(y_hl[:, 1, 2 * n:2 * n + 2, :].rearrange("p t f -> p (t f)"), a_bank[:, 0:2 * F], Y_DOWN,
                         y_hl[:, 0, 2 * n:2 * n + 2, :].rearrange("p t f -> p (t f)")).then_inc(v_y, 1)

            def unit_lo(load):
                slot = loads[load][2]
                dve.wait_ge(a_unit, load + 1)
                minus_hi(split[slot][:, 1, :], raw[load % RAW_RING], col["s_a"], split[slot][:, 0, :]).then_inc(v_unit, 1)

            for s in range(NS + LAG + 4):
                j, b = divmod(s, NB)
                e = s - EXP_LAG
                if 0 <= e < NS:
                    subtract_max(e)
                if s < NS:
                    add_adj(s)
                    if b == 0 and j >= 1:
                        max_diagonals(j - 1)
                    running_max(s)
                    if b == NB - 1:
                        fold_max(j)
                elif s == NS:
                    max_diagonals(j - 1)
                if 0 <= e < NS:
                    p_lo(e)
                if s < NS:
                    adj_maximum(s)
                if 2 <= b < 2 + IT and j >= 2:
                    attention_rows(j - 2, b - 2)
                if b == 2 + IT and j >= 2:
                    normalise(j - 2)
                if s == NS:
                    dve.tensor_reduce(col["st_a"], adj_all[:, :], AX, ALU.max).then_inc(v_st, 1)
                    dve.wait_ge(a_w1, 1)
                    minus_hi(w1_hl[:, 1, :, :].rearrange("p k f -> p (k f)"), w1_raw, col["s_w1"],
                             w1_hl[:, 0, :, :].rearrange("p k f -> p (k f)")).then_inc(v_w1, 1)
                if s == NS + 4:
                    dve.wait_ge(g_ar, 3)
                    power(col["e_a"], col["mx_a"])
                    scale_of(col["s_a"], col["e_a"])
                    dve.tensor_scalar(col["inv_h"], col["e_a"], col["e_w1"], 1 / (TOP * TOP * X1_UP * Y_DOWN),
                                      ALU.mult, ALU.mult).then_inc(v_sa, 1)
                y = s - Y_FIRST
                if 0 < y < NT // 2:
                    y_lo(y - 1)
                if 0 <= y < NT // 2 - 1:
                    x1_lo(2 * y)
                    x1_lo(2 * y + 1)
                if NS + LAG - EARLY <= s < NS + LAG:
                    unit_lo(s - (NS + LAG - EARLY))

            def o_stats(n):
                o = o_row[n % O_RING]
                dve.wait_ge(p_o, n + 1)
                dve.wait_ge(g_res, n + 1)
                if n >= O_RING:
                    dve.wait_ge(d_out[n % O_RING], 16 * (n // O_RING))
                dve.tensor_tensor(o, o_bank[n % 3][:, :], x1_res[n % O_RING], ALU.add).then_inc(v_or, 1)
                dve.wait_ge(v_or, n + 1)
                link(dve.bn_stats(bn[:, :], o))
                link(dve.bn_aggr(mv[:, n % 2, :], bn[:, :]))
                dve.tensor_scalar(veps[:, n % 2:n % 2 + 1], mv[:, n % 2, 1:2], EPS, None, ALU.add).then_inc(v_ovar, 1)

            def o_normalise(n):
                dve.wait_ge(g_orstd, n + 1)
                o = o_row[n % O_RING]
                dve.tensor_scalar(o, o, mv[:, n % 2, 0:1], rstd[:, n % 2:n % 2 + 1], ALU.subtract, ALU.mult).then_inc(v_o, 1)

            def h_maximum(n):
                dve.wait_ge(a_h, n + 1)
                link(abs_max(h_max[:, n:n + 1], hT[:, CW * n:CW * (n + 1)]))

            for n, (conv, k, ic, b, _) in enumerate(units):
                for load in split_at[n]:
                    unit_lo(load)
                if conv == k == 0 and b == Y_LAST[0]:
                    x1_lo(NT - 2)
                    x1_lo(NT - 1)
                if conv == k == 0 and b == Y_LAST[1]:
                    y_lo(NT // 2 - 1)
                if conv == 0 and k >= 1 and b == OUT_AT:
                    h_maximum(k - 1)
                if conv == 1 and k == 0 and b == 0:
                    h_maximum(NC - 1)
                    link(dve.tensor_reduce(col["t0"], h_max[:, :], AX, ALU.max))
                    power(col["e_h"], col["t0"])
                    scale_of(col["s_h"], col["e_h"])
                    link(dve.tensor_scalar(col["inv_z"], col["e_h"], col["e_a"], 1 / TOP ** 2, ALU.mult, ALU.mult))
                    for g in range(NC):
                        dve.tensor_scalar(hT[:, CW * g:CW * (g + 1)], hT[:, CW * g:CW * (g + 1)], col["s_h"], None,
                                          ALU.mult).then_inc(v_h, 1)
                    for g in range(NC):
                        dve.wait_ge(a_ht, g + 1)
                        minus_hi(h_hl[:, 1, TW * g:TW * (g + 1), :].rearrange("p t f -> p (t f)"), ht_bank[g % 3][:, :], 1.0,
                                 h_hl[:, 0, TW * g:TW * (g + 1), :].rearrange("p t f -> p (t f)")).then_inc(v_ht, 1)
                if conv == 1 and k >= 1:
                    if b - 1 in O_AT:
                        o_stats(TW * (k - 1) + O_AT.index(b - 1))
                    if b - 2 in O_AT:
                        o_normalise(TW * (k - 1) + O_AT.index(b - 2))
            for n in range(NT - TW, NT):
                o_stats(n)
                o_normalise(n)

        @block.gpsimd
        def _(pool):
            pool.memset(ident[:, :], 0.0).then_inc(g_id, 1)
            pool.memset(ones[:, :], 1.0)
            pool.memset(col["minus_half"], -0.5)
            pool.wait_ge(g_id, 1)
            pool.affine_select(out=ident[:, :], in_=ident[:, :], compare_op=ALU.not_equal, fill=1.0, base=0,
                               pattern=[[-1, P]], channel_multiplier=1).then_inc(g_id, 1)
            pool.wait_ge(v_st, 5)
            pool.partition_all_reduce(cols("mx_m", "mx_gb"), cols("st_m", "st_gb"), P, ALL_MAX).then_inc(g_ar, 1)
            pool.wait_ge(v_st, 6)
            pool.partition_all_reduce(col["mx_x"], col["st_x"], P, ALL_MAX).then_inc(g_ar, 1)
            for s in range(NS + LAG + 4):
                e = s - EXP_LAG
                if 0 <= e < NS:
                    i, b = divmod(e, NB)
                    pool.wait_ge(a_exp, e + 1)
                    if b == 0 and i >= 1:
                        pool.wait_ge(p_den, i)
                    if b == 0:
                        pool.tensor_copy(den[:, :], ring[:, e % RING, :]).then_inc(g_den, 1)
                    else:
                        pool.wait_ge(g_den, e)
                        pool.tensor_tensor(den[:, :], den[:, :], ring[:, e % RING, :], ALU.add).then_inc(g_den, 1)
                if s % NB == 1 + IT and s // NB >= 2:
                    i = s // NB - 2
                    pool.wait_ge(v_var, i + 1)
                    for t in range(IT):
                        last = pool.tensor_tensor(rstd[:, t:t + 1], veps[:, t:t + 1], col["minus_half"], ALU.pow)
                    last.then_inc(g_rstd, 1)
                if s == NS + 1:
                    pool.wait_ge(v_st, 7)
                    pool.partition_all_reduce(col["mx_a"], col["st_a"], P, ALL_MAX).then_inc(g_ar, 1)

            def tile_of(n):
                return TW * ORDER[1][n // TW] + n % TW

            def load_residual(n):
                t = tile_of(n)
                pool.dma_start(x1_res[n % O_RING], x1_dram[P * t:P * (t + 1), :]).then_inc(d_res[n % O_RING], 16)

            pool.wait_ge(d_x1, 16 * NI)
            pool.wait_ge(p_y, NT // 2)
            for n in range(O_RING):
                load_residual(n)
            pool.wait_ge(d_late, 32)
            for n in range(NT + 1):
                if n < NT:
                    pool.wait_ge(d_res[n % O_RING], 16 * (n // O_RING + 1))
                    pool.tensor_tensor(x1_res[n % O_RING], x1_res[n % O_RING], b2_row, ALU.add).then_inc(g_res, 1)
                    pool.wait_ge(v_ovar, n + 1)
                    pool.tensor_tensor(rstd[:, n % 2:n % 2 + 1], veps[:, n % 2:n % 2 + 1], col["minus_half"],
                                       ALU.pow).then_inc(g_orstd, 1)
                if n >= 1:
                    t = tile_of(n - 1)
                    pool.wait_ge(v_o, n)
                    pool.dma_start(out[P * t:P * (t + 1), :], o_row[(n - 1) % O_RING]).then_inc(d_out[(n - 1) % O_RING], 16)
                    if n - 1 + O_RING < NT:
                        load_residual(n - 1 + O_RING)
            for i in range(O_RING):
                pool.wait_ge(d_out[i], 16 * (NT // O_RING))


_INPUTS = ["x", "adj", "L0_gnn_Wq", "L0_gnn_bq", "L0_gnn_Wk", "L0_gnn_bk", "L0_gnn_Wv", "L0_gnn_bv",
           "L1_gnn_W1", "L1_gnn_b1", "L1_gnn_W2", "L1_gnn_b2"]


def kernel(**inputs):
    import numpy as np
    import concourse.bacc as bacc
    from concourse.bass_utils import run_bass_kernel_spmd

    nc = bacc.Bacc("TRN2", target_bir_lowering=False, num_devices=1)
    arrays = {f"in_{name}": np.ascontiguousarray(inputs[name]) for name in _INPUTS}
    args = [nc.dram_tensor(name, a.shape, mybir.dt.from_np(a.dtype), kind="ExternalInput").ap() for name, a in arrays.items()]
    out = nc.dram_tensor("out", (N, D), F32, kind="ExternalOutput").ap()
    x1_dram = nc.dram_tensor("x1_dram", (N, D), F32, kind="Internal").ap()
    g_dram = nc.dram_tensor("g_dram", (NI, P, 2 * KD * IW), F16, kind="Internal").ap()
    at_dram = nc.dram_tensor("at_dram", (NS, P, BANK), F32, kind="Internal").ap()
    gnn_program(nc, *args, out, x1_dram, g_dram, at_dram)
    return run_bass_kernel_spmd(nc, [arrays], core_ids=[0]).results[0]["out"]
```

```python
import math
from contextlib import ExitStack

import concourse.bass as bass
from concourse import mybir

F32 = mybir.dt.float32
F16 = mybir.dt.float16
BF16 = mybir.dt.bfloat16
U32 = mybir.dt.uint32
ALU = mybir.AluOpType
ACT = mybir.ActivationFunctionType
AX = mybir.AxisListType.X
ALL_MAX = bass.bass_isa.ReduceOp.max

P = 128
N, D, F = 4096, 512, 128
KD = D // P
NT = N // P
BANK = 512
XG = 4
IW = 256
IT = IW // P
NI = N // IW
NB = N // IW
NS = NI * NB
RING = 20
LAG = NB + 2
EXP_LAG = LAG - 1
STAGE = 3
ADJ_RING = 2
U_BANKS = 2 * IT
WVT_BLOCKS = M_BLOCKS = (2, 3, 0, 1)
EPS = 1e-5

TOP = 2.0 ** 13
TINY = 2.0 ** -40
EXP_BITS = 0x7F800000
LOGIT = 0.5 / math.sqrt(D)
P_UP = 2.0 ** 12
X1_UP = 2.0 ** 10
Y_DOWN = 2.0 ** -18

X1_RING = 8
Y_FIRST = NS + 1
CW = 2 * IW
NC = N // CW
UNITS = NC * NB
UNIT = 2 * IT * IW
RAW_RING = 6
SLOTS = 33
Z_RING = 2
H_BANKS = 3
O_RING = 4
TW = CW // P
ORDER = [list(range(NC)), list(range(NC))[::-1]]
PLAIN_SLOTS = 4
EARLY = 14
Y_LAST = (5, 9)
LEAD = 4
OUT_AT = 1
O_AT = (4, 7, 10, 13)
STATS_DELAY, NORM_DELAY, STORE_DELAY = 1, 5, 6


def unit_plan():
    units, loads, slot_of = [], [], {}
    free = [(0, slot) for slot in range(SLOTS)]
    for conv in range(2):
        for k, ic in enumerate(ORDER[conv]):
            for b in range(NB):
                n = len(units)
                load = None
                if conv == 0 or (ic, b) not in slot_of:
                    after, slot_of[ic, b] = free.pop(0)
                    load = len(loads)
                    loads.append((ic, b, slot_of[ic, b], after))
                units.append((conv, k, ic, b, load))
                if conv or n < UNITS - SLOTS:
                    free.append((n + 1, slot_of.pop((ic, b))))
    split_at = [[] for _ in units]
    busy = UNITS + NB - 2
    for first, end, start, stop in ((EARLY, UNITS, 0, UNITS - 1), (UNITS, busy, UNITS + 2, UNITS + NB),
                                    (busy, len(loads), UNITS + NB, 2 * UNITS - LEAD)):
        for load in range(first, end):
            split_at[start + (load - first) * (stop - start) // (end - first)].append(load)
    own = {u[4]: n for n, u in enumerate(units)}
    for n, ls in enumerate(split_at):
        assert all(loads[l][3] <= n and own[l] >= n for l in ls)
    return units, loads, split_at


def output_plan(delay):
    at = [[] for _ in range(2 * UNITS + 1)]
    for n in range(NT):
        at[min(UNITS + NB * (n // TW + 1) + O_AT[n % TW] + delay, 2 * UNITS)].append(n)
    return at


def output_rows(n):
    t = TW * ORDER[1][n // TW] + n % TW
    return slice(P * t, P * (t + 1))


def gnn_program(nc, x, adj, wq, bq, wk, bk, wv, bv, w1, b1, w2, b2, out, x1_dram, g_dram, at_dram):
    with ExitStack() as ctx:
        def sb(name, shape, dt):
            return ctx.enter_context(nc.sbuf_tensor(name, shape, dt))

        def sem(name):
            return ctx.enter_context(nc.semaphore(name))

        xT = sb("xT", [P, 2, KD * N], F16)
        xv = sb("xv", [P, NT, D], F32)
        ring = sb("ring", [P, RING, BANK], F32)
        gT = sb("gT", [P, 2, 2 * KD * IW], F16)
        adj_in = sb("adj_in", [P, ADJ_RING, IT, 2 * IW], F32)
        stage = sb("stage", [P, STAGE, BANK], F32)
        pT = sb("pT", [P, 2, 2, BANK], F16)
        xr = sb("xr", [P, IT, D], F32)
        run_max = sb("run_max", [P, BANK], F32)
        den = sb("den", [P, BANK], F32)
        fold = sb("fold", [P, IW], F32)
        max_row = sb("max_row", [P, IW], F32)
        ident = sb("ident", [P, P], F32)
        ones = sb("ones", [P, P], F32)
        adj_max = sb("adj_max", [P, NB], F32)
        adj_all = sb("adj_all", [P, NI], F32)
        c_all = sb("c_all", [P, NT], F32)
        bq_c = sb("bq_c", [P, KD], F32)
        bk_c = sb("bk_c", [P, KD], F32)
        gb_c = sb("gb_c", [P, KD], F32)
        b1_c = sb("b1_c", [P, 1], F32)
        x_max = sb("x_max", [P, NT // XG], F32)
        q_max = sb("q_max", [P, IT], F32)
        bn = sb("bn", [P, 6], F32)
        mv = sb("mv", [P, O_RING, 2], F32)
        veps = sb("veps", [P, O_RING], F32)
        rstd = sb("rstd", [P, O_RING], F32)
        h_max = sb("h_max", [P, NC], F32)
        shift = sb("shift", [P, O_RING], F32)
        minus_mean = sb("minus_mean", [P, O_RING], F32)
        names = ["m0", "m1", "m2", "m3", "st_m", "st_wv", "st_w1", "st_gb", "mx_m", "mx_wv", "mx_w1", "mx_gb",
                 "e_m", "e_wv", "e_w1", "s_m", "s_wv", "s_w1", "mx_bv", "st_x", "mx_x", "e_x", "s_x", "k_g", "k_v",
                 "bound", "e_v", "s_v", "e_g", "s_g", "k_gs", "k_u", "k_l", "c0", "t0", "t1", "st_a", "mx_a",
                 "e_a", "s_a", "inv_h", "e_h", "s_h", "inv_z", "minus_half", "minus_one"]
        sc = sb("sc", [P, len(names)], F32)
        col = {name: sc[:, i:i + 1] for i, name in enumerate(names)}

        def cols(first, last):
            return sc[:, names.index(first):names.index(last) + 1]

        def flat(ap):
            return ap.rearrange("p a b -> p (a b)")

        def xt_block(part, k, tile, width=P):
            return xT[:, part, k * N + tile * P:k * N + tile * P + width]

        xt_tiles = [xT[:, part, :].rearrange("p (k n) -> p k n", k=KD) for part in range(2)]
        v_hl = xv[:, :, :].bitcast(F16).rearrange("p t (two d) -> p t two d", two=2)
        wq_raw, wk_raw, wv_raw = (ring[:, KD * i:KD * (i + 1), :] for i in range(3))
        wvT = flat(ring[:, 12:16, :]).bitcast(F16).rearrange("p (two k e) -> p two k e", two=2, k=KD)
        m_hl = flat(ring[:, 16:20, :]).bitcast(F16).rearrange("p (two k e) -> p two k e", two=2, k=KD)
        g_out = [flat(ring[:, 4 * i:4 * (i + 1), :]).bitcast(F16).rearrange("p (two k n) -> p two k n", two=2, k=KD)
                 for i in range(2)]
        p_flat = pT[:, :, :, :].rearrange("p a b c -> p (a b c)").bitcast(F32)
        c_row, bv_row = p_flat[:, 0:D], p_flat[:, D:2 * D]
        v_row = [xr[:, i, :] for i in range(2)]
        g_row = [stage[:, i, :] for i in range(2)]
        unused = stage[:, 2, :].bitcast(BF16)[:, 0:D]
        w1_stat = flat(adj_in[:, 0, :, :])[:, 0:KD * F]
        xt_f32 = flat(xT[:, :, :]).bitcast(F32)
        x1_in = [xt_f32[:, D * i:D * (i + 1)] for i in range(X1_RING)]
        hT = xt_f32[:, 0:N]
        y_hl = xt_f32[:, N:2 * N].bitcast(F16).rearrange("p (two t f) -> p two t f", two=2, t=NT)
        raw = [xt_f32[:, 2 * N + UNIT * i:2 * N + UNIT * (i + 1)] for i in range(RAW_RING)]
        rest = xt_f32[:, 2 * N + UNIT * RAW_RING:]
        w1_raw = rest[:, 0:KD * F]
        w1_hl = rest[:, D:2 * D].bitcast(F16).rearrange("p (two k f) -> p two k f", two=2, k=KD)
        x1T = [rest[:, D * (2 + i):D * (3 + i)].bitcast(F16).rearrange("p (two n) -> p two n", two=2) for i in range(2)]
        pairs = [ring[:, i % RING:i % RING + 2, :] for i in range(NS - RING, NS, 2)]
        split = [flat(gT[:, :, :])[:, 2 * UNIT * i:2 * UNIT * (i + 1)] for i in range(2)]
        split += [flat(adj_in[:, i, :, :]).bitcast(F16) for i in range(2)]
        split += [flat(pair).bitcast(F16) for pair in pairs]
        split += [flat(xv[:, 2 * i:2 * (i + 1), :]).bitcast(F16) for i in range(NT // 2)]
        split += [pT[:, :, :, :].rearrange("p a b c -> p (a b c)"), flat(stage[:, 0:2, :]).bitcast(F16),
                  flat(xr[:, :, :]).bitcast(F16)]
        split = [a.rearrange("p (two n) -> p two n", two=2) for a in split]
        assert len(split) == SLOTS
        h_hl = y_hl
        ht_place = [hT[:, D * i:D * (i + 1)] for i in range(8)]
        z_f, o_row, w2_s, b2_row = ht_place[0:2], ht_place[2:6], ht_place[6], ht_place[7]
        x1_res = [rest[:, D * i:D * (i + 1)] for i in range(O_RING)]

        bank = [ctx.enter_context(nc.psum_tensor(f"bank{i}", [P, BANK], F32)) for i in range(8)]
        s_bank, a_bank, misc, u_bank = bank[0:2], bank[2], bank[3], bank[4:8]
        m_bank = [bank[0], bank[1], bank[4], bank[5]]
        wvt_bank = [bank[7], bank[6], bank[2], bank[3]]
        xt_bank = [bank[2], bank[3]]
        v_bank = [bank[6], bank[7], bank[4], bank[5]]
        acc_bank = bank[4:6]
        ht_bank = bank[0:3]
        o_bank = [bank[6], bank[7], bank[3]]

        d_small, d_wq, d_wk, d_wv, d_w1, d_late, d_x1 = (
            sem(s) for s in ("d_small", "d_wq", "d_wk", "d_wv", "d_w1", "d_late", "d_x1"))
        d_x = [sem(f"d_xgroup{i}") for i in range(NT // XG)]
        d_gout = [sem(f"d_gout{i}") for i in range(2)]
        d_gt = [sem(f"d_gt{i}") for i in range(2)]
        d_adj = [sem(f"d_adj{i}") for i in range(ADJ_RING)]
        d_at = [sem(f"d_at{i}") for i in range(STAGE)]
        d_xr = sem("d_xr")
        d_x1in = [sem(f"d_x1in{i}") for i in range(X1_RING)]
        d_raw = [sem(f"d_raw{i}") for i in range(RAW_RING)]
        d_res = [sem(f"d_res{i}") for i in range(O_RING)]
        d_out = [sem(f"d_out{i}") for i in range(O_RING)]
        p_pre, p_xt, p_v, p_g, p_at, p_qk, p_mt, p_mr, p_pv, p_den, p_x1t, p_y, p_unit, p_ht, p_o = (
            sem("p_" + s) for s in "pre xt v g at qk mt mr pv den x1t y unit ht o".split())
        a_pre, a_bias, a_xt, a_v, a_gf, a_g, a_at, a_exp, a_p, a_mr, a_w1, a_x1t, a_y, a_unit, a_h, a_ht, a_z, a_o = (
            sem("a_" + s) for s in "pre bias xt v gf g at exp p mr w1 x1t y unit h ht z o".split())
        v_st, v_sc, v_sx, v_pre, v_xt, v_c, v_vf, v_v, v_g, v_add, v_run, v_fold, v_diag, v_sub, v_p, v_abs = (
            sem("v_" + s) for s in "st sc sx pre xt c vf v g add run fold diag sub p abs".split())
        v_r, v_var, v_x1, v_w1, v_x1t, v_y, v_sa, v_scales, v_unit, v_hmax, v_h, v_ht, v_or, v_ovar, v_chain = (
            sem("v_" + s) for s in "r var x1 w1 x1t y sa scales unit hmax h ht or ovar chain".split())
        g_id, g_ar, g_den, g_rstd, g_res, g_norm, g_orstd = (sem("g_" + s) for s in "id ar den rstd res norm orstd".split())

        units, loads, split_at = unit_plan()
        block = ctx.enter_context(nc.Block())

        @block.sync
        def _(sp):
            sp.dma_start(bq_c[:, :], bq.rearrange("(p k) -> p k", k=KD)).then_inc(d_small, 16)
            sp.dma_start(bk_c[:, :], bk.rearrange("(p k) -> p k", k=KD)).then_inc(d_small, 16)
            sp.dma_start(b1_c[:, :], b1.rearrange("(p o) -> p o", o=1)).then_inc(d_small, 16)
            sp.dma_start(wq_raw, wq.rearrange("(p k) d -> p k d", k=KD)).then_inc(d_wq, 16)
            sp.dma_start(wk_raw, wk.rearrange("(p k) d -> p k d", k=KD)).then_inc(d_wk, 16)
            sp.dma_start(bv_row, bv.rearrange("(o d) -> o d", o=1).broadcast_to([P, D])).then_inc(d_small, 16)
            sp.dma_start(w1_stat, w1.rearrange("(p k) f -> p (k f)", k=KD)).then_inc(d_small, 16)
            sp.dma_start(wv_raw, wv.rearrange("(k p) d -> p k d", p=P)).then_inc(d_wv, 16)
            x_tiles = x.rearrange("(t p) d -> p t d", p=P)
            for i in range(NT // XG):
                sp.dma_start(xv[:, XG * i:XG * (i + 1), :], x_tiles[:, XG * i:XG * (i + 1), :]).then_inc(d_x[i], 16)

            def load_adj(q):
                i, b = divmod(2 * q, NB)
                sp.dma_start(adj_in[:, q % ADJ_RING, :, :],
                             adj[IW * i:IW * (i + 1), IW * b:IW * (b + 2)].rearrange("(t p) c -> p t c", p=P)
                             ).then_inc(d_adj[q % ADJ_RING], 16)

            def load_gt(i):
                sp.dma_start(gT[:, i % 2, :], g_dram[i]).then_inc(d_gt[i % 2], 16)

            sp.wait_ge(v_st, 2)
            for q in range(ADJ_RING):
                load_adj(q)
            for g in range(NT // XG):
                sp.wait_ge(a_g, KD * (g + 1))
                sp.wait_ge(v_g, KD * (g + 1))
                for i in range(2):
                    sp.dma_start(g_dram[2 * g + i].rearrange("p (a n) -> p a n", n=IW),
                                 g_out[g % 2].rearrange("p a b n -> p (a b) n")[:, :, IW * i:IW * (i + 1)]
                                 ).then_inc(d_gout[g % 2], 16)
                if g == 1:
                    sp.wait_ge(d_gout[0], 32)
                    load_gt(0)
                    load_gt(1)
            sp.wait_ge(v_vf, NT)
            sp.wait_ge(a_v, NT)
            sp.wait_ge(v_v, NT)
            x_chunks = x.rearrange("(i t p) d -> i p t d", t=IT, p=P)
            x1_chunks = x1_dram.rearrange("(i t p) d -> i p t d", t=IT, p=P)
            sp.dma_start(xr[:, :, :], x_chunks[0]).then_inc(d_xr, 16)
            for g in range(2):
                sp.wait_ge(d_gout[g], 32 * (NT // XG // 2))

            def load_raw(l):
                ic, b = loads[l][:2]
                if l >= RAW_RING:
                    sp.wait_ge(a_unit, l - RAW_RING + 1)
                    sp.wait_ge(v_unit, l - RAW_RING + 1)
                sp.dma_start(raw[l % RAW_RING].rearrange("p (i c) -> p i c", i=2),
                             at_dram.rearrange("(c i b) p n -> c b p i n", i=2, b=NB)[ic, b]
                             ).then_inc(d_raw[l % RAW_RING], 16)

            def load_x1(t):
                if t >= X1_RING:
                    sp.wait_ge(p_x1t, t - X1_RING + 1)
                sp.dma_start(x1_in[t % X1_RING], x1_dram[P * t:P * (t + 1), :]).then_inc(d_x1in[t % X1_RING], 16)

            x1_loads = 0
            for s in range(NS + LAG + 4):
                if s < NS:
                    sp.wait_ge(a_at, s + 1)
                    sp.dma_start(at_dram[s], stage[:, s % STAGE, :]).then_inc(d_at[s % STAGE], 16)
                    if s % 2 and s // 2 + ADJ_RING < NS // 2:
                        sp.wait_ge(p_at, s + 1)
                        load_adj(s // 2 + ADJ_RING)
                    i, b = divmod(s, NB)
                    if b == 0 and 1 <= i < NI - 1:
                        sp.wait_ge(p_qk, s)
                        load_gt(i + 1)
                j, b = divmod(s, NB)
                if b == 5 and 2 <= j < NI + 1:
                    sp.wait_ge(v_x1, j - 1)
                    sp.dma_start(x1_chunks[j - 2], xr[:, :, :]).then_inc(d_x1, 16)
                if b == 7 and 2 <= j < NI + 1:
                    sp.wait_ge(d_x1, 16 * (j - 1))
                    sp.dma_start(xr[:, :, :], x_chunks[j - 1]).then_inc(d_xr, 16)
                if s == NS:
                    sp.wait_ge(p_qk, NS)
                    sp.dma_start(w1_raw, w1.rearrange("(k p) f -> p k f", p=P)).then_inc(d_w1, 16)
                    for t in range(X1_RING):
                        load_x1(t)
                    x1_loads = X1_RING
                    for i in range(STAGE):
                        sp.wait_ge(d_at[i], 16 * len(range(i, NS, STAGE)))
                    for l in range(RAW_RING):
                        load_raw(l)
                if NS + LAG - EARLY <= s < NS + LAG:
                    load_raw(RAW_RING + s - (NS + LAG - EARLY))
                if s > Y_FIRST:
                    for _ in range(2):
                        if x1_loads < NT - 2 and (x1_loads < NT - 4 or s >= NS + 7):
                            load_x1(x1_loads)
                            x1_loads += 1
            sp.wait_ge(v_x1, NI)
            sp.dma_start(x1_chunks[NI - 1], xr[:, :, :]).then_inc(d_x1, 16)

            for ls in split_at:
                for load in ls:
                    if load == UNITS + NC:
                        sp.wait_ge(p_ht, NC)
                        sp.dma_start(w2_s, w2[:, :]).then_inc(d_late, 16)
                        sp.dma_start(b2_row, b2.rearrange("(o d) -> o d", o=1).broadcast_to([P, D])).then_inc(d_late, 16)
                    if load + RAW_RING < len(loads):
                        load_raw(load + RAW_RING)

        @block.tensor
        def _(pe):
            def product(dst, pairs):
                for i, (ah, al, bh, bl) in enumerate(pairs):
                    pe.matmul(dst, ah, bh, start=(i == 0), stop=False)
                    pe.matmul(dst, ah, bl, start=False, stop=False)
                    last = pe.matmul(dst, al, bh, start=False, stop=(i == len(pairs) - 1))
                return last

            def accumulate(dst, pairs):
                for i, (a, b) in enumerate(pairs):
                    last = pe.matmul(dst, a, b, start=(i == 0), stop=(i == len(pairs) - 1))
                return last

            pe.wait_ge(d_wq, 16)
            pe.wait_ge(d_wk, 16)
            for k in range(KD):
                accumulate(m_bank[k][:, :], [(wq_raw[:, e, P * k:P * (k + 1)], wk_raw[:, e, :]) for e in range(KD)]
                           ).then_inc(p_pre, 1)
            pe.wait_ge(d_small, 16 * 5)
            for k in range(KD):
                last = accumulate(bank[2][:, k:k + 1], [(wk_raw[:, e, P * k:P * (k + 1)], bq_c[:, e:e + 1]) for e in range(KD)])
            last.then_inc(p_pre, 1)
            everywhere = [P, P]
            accumulate(bank[3][:, :], [(bk_c[:, e:e + 1].broadcast_to(everywhere), wq_raw[:, e, :]) for e in range(KD)]
                       ).then_inc(p_pre, 1)
            accumulate(bank[6][:, 0:1], [(bq_c[:, e:e + 1].broadcast_to(everywhere), bk_c[:, e:e + 1]) for e in range(KD)]
                       ).then_inc(p_pre, 1)
            pe.wait_ge(g_id, 2)
            pe.wait_ge(d_wv, 16)
            for k in range(KD):
                if k == 1:
                    pe.wait_ge(a_bias, 2)
                    pe.wait_ge(v_pre, 1)
                for e in range(KD):
                    last = pe.transpose(wvt_bank[k][:, P * e:P * (e + 1)], wv_raw[:, e, P * k:P * (k + 1)], ident[:, :])
                last.then_inc(p_pre, 1)

            def weights_split(n):
                pe.wait_ge(a_pre, n)
                pe.wait_ge(v_pre, 1 + n)

            def x_transpose(t):
                pe.wait_ge(d_x[t // XG], 16)
                if t < 2:
                    weights_split(t + 1)
                if t >= 2:
                    pe.wait_ge(a_xt, t - 1)
                    pe.wait_ge(v_xt, t - 1)
                for k in range(KD):
                    last = pe.transpose(xt_bank[t % 2][:, P * k:P * (k + 1)], xv[:, t, P * k:P * (k + 1)], ident[:, :])
                last.then_inc(p_xt, 1)

            x_transpose(0)
            for t in range(NT):
                if t + 1 < NT:
                    x_transpose(t + 1)
                pe.wait_ge(a_xt, t + 1)
                pe.wait_ge(v_xt, t + 1)
                if t == 0:
                    weights_split(KD)
                elif 2 <= t < U_BANKS:
                    weights_split(KD + t - 1)
                elif t >= U_BANKS:
                    pe.wait_ge(v_vf, t - U_BANKS + 1)
                product(v_bank[t % U_BANKS][:, :],
                        [(xt_block(0, k, t), xt_block(1, k, t), wvT[:, 0, k, :], wvT[:, 1, k, :]) for k in range(KD)]
                        ).then_inc(p_v, 1)
                if t % XG == XG - 1:
                    first = t - XG + 1
                    if first == 0:
                        weights_split(2 * KD)
                    for kk in range(KD):
                        n = KD * (t // XG) + kk
                        if n >= 2:
                            pe.wait_ge(a_gf, n - 1)
                        product(s_bank[n % 2][:, :],
                                [(m_hl[:, 0, k, P * kk:P * (kk + 1)], m_hl[:, 1, k, P * kk:P * (kk + 1)],
                                  xt_block(0, k, first, BANK), xt_block(1, k, first, BANK)) for k in range(KD)]
                                ).then_inc(p_g, 1)
            pe.wait_ge(a_gf, NT // XG * KD)
            pe.wait_ge(v_vf, NT)

            def adj_transpose(s):
                q = s // 2
                pe.wait_ge(d_adj[q % ADJ_RING], 16 * (q // ADJ_RING + 1))
                if s >= 1:
                    pe.wait_ge(a_at, s)
                for jj in range(IT):
                    for t in range(IT):
                        c = IW * (s % 2) + P * jj
                        last = pe.transpose(a_bank[:, IW * jj + P * t:IW * jj + P * (t + 1)],
                                            adj_in[:, q % ADJ_RING, t, c:c + P], ident[:, :])
                last.then_inc(p_at, 1)

            def logits(s):
                i, b = divmod(s, NB)
                if b == 0:
                    pe.wait_ge(d_gt[i % 2], 16 * (i // 2 + 1))
                if s >= 2:
                    pe.wait_ge(v_add, s - 1)
                g = gT[:, i % 2, :].rearrange("p (two k n) -> p two k n", two=2, k=KD)
                for jj in range(IT):
                    last = product(s_bank[s % 2][:, IW * jj:IW * (jj + 1)],
                                   [(xt_block(0, k, IT * b + jj), xt_block(1, k, IT * b + jj), g[:, 0, k, :], g[:, 1, k, :])
                                    for k in range(KD)])
                last.then_inc(p_qk, 1)

            def max_transpose(i):
                pe.wait_ge(v_fold, i + 1)
                if i >= 2:
                    pe.wait_ge(v_r, IT * (i - 1))
                for t in range(IT):
                    last = pe.transpose(misc[:, P * t:P * (t + 1)], fold[:, P * t:P * (t + 1)], ident[:, :])
                last.then_inc(p_mt, 1)

            def max_to_row(i):
                pe.wait_ge(v_diag, i + 1)
                pe.matmul(misc[:, 0:IW], ones[:, :], fold[:, :], start=True, stop=True).then_inc(p_mr, 1)

            def attend(s):
                i, b = divmod(s, NB)
                pe.wait_ge(a_p, s + 1)
                pe.wait_ge(v_p, s + 1)
                if s == 0:
                    pe.wait_ge(a_v, NT)
                    pe.wait_ge(v_v, NT)
                if b == 0 and i >= 2:
                    pe.wait_ge(v_r, IT * (i - 1))
                for t in range(IT):
                    dst = u_bank[IT * (i % 2) + t][:, :]
                    for jj in range(IT):
                        c = IW * jj + P * t
                        ah, al = pT[:, s % 2, 0, c:c + P], pT[:, s % 2, 1, c:c + P]
                        vh, vl = v_hl[:, IT * b + jj, 0, :], v_hl[:, IT * b + jj, 1, :]
                        end = b == NB - 1 and jj == IT - 1
                        pe.matmul(dst, ah, vh, start=(b == 0 and jj == 0), stop=False)
                        pe.matmul(dst, ah, vl, start=False, stop=False)
                        last = pe.matmul(dst, al, vh, start=False, stop=end)
                last.then_inc(p_pv, 1)

            def denominators(i):
                pe.wait_ge(g_den, NB * (i + 1))
                pe.wait_ge(a_mr, min(i + 2, NI))
                for t in range(IT):
                    last = accumulate(misc[:, t:t + 1], [(den[:, IW * jj + P * t:IW * jj + P * (t + 1)], ones[:, 0:1])
                                                         for jj in range(IT)])
                last.then_inc(p_den, 1)

            def x1_transpose(t):
                if t < NT - IT:
                    pe.wait_ge(d_x1in[t % X1_RING], 16 * (t // X1_RING + 1))
                    src = x1_in[t % X1_RING]
                else:
                    pe.wait_ge(v_x1, NI)
                    src = xr[:, t - (NT - IT), :]
                if t >= 2:
                    pe.wait_ge(a_x1t, t - 1)
                    pe.wait_ge(v_x1t, t - 1)
                for k in range(KD):
                    last = pe.transpose(bank[t % 2][:, P * k:P * (k + 1)], src[:, P * k:P * (k + 1)], ident[:, :])
                last.then_inc(p_x1t, 1)

            def y_rows(n):
                pe.wait_ge(a_x1t, 2 * n + 2)
                pe.wait_ge(v_x1t, 2 * n + 2)
                pe.wait_ge(a_w1, 1)
                pe.wait_ge(v_w1, 1)
                if n >= 1:
                    pe.wait_ge(a_y, n)
                    pe.wait_ge(v_y, n)
                for i in range(2):
                    last = product(a_bank[:, F * i:F * (i + 1)],
                                   [(x1T[i][:, 0, P * k:P * (k + 1)], x1T[i][:, 1, P * k:P * (k + 1)],
                                     w1_hl[:, 0, k, :], w1_hl[:, 1, k, :]) for k in range(KD)])
                last.then_inc(p_y, 1)

            for s in range(NS + LAG):
                j, b = divmod(s, NB)
                if s < NS:
                    adj_transpose(s)
                    logits(s)
                if b == 0 and 1 <= j <= NI:
                    max_transpose(j - 1)
                y = s - Y_FIRST
                if 0 < y < NT // 2:
                    y_rows(y - 1)
                if 0 <= y < NT // 2 - 1:
                    if y == 0:
                        pe.wait_ge(v_add, NS)
                        pe.wait_ge(a_at, NS)
                    x1_transpose(2 * y)
                    x1_transpose(2 * y + 1)
                if s >= LAG:
                    attend(s - LAG)
                if b == 0 and 1 <= j <= NI:
                    max_to_row(j - 1)
                if b == 1 and j >= 2:
                    denominators(j - 2)

            def h_transpose(g):
                pe.wait_ge(v_h, g + 1)
                if g >= H_BANKS:
                    pe.wait_ge(a_ht, g - H_BANKS + 1)
                    pe.wait_ge(v_ht, g - H_BANKS + 1)
                for i in range(TW):
                    last = pe.transpose(ht_bank[g % H_BANKS][:, P * i:P * (i + 1)],
                                        hT[:, CW * g + P * i:CW * g + P * (i + 1)], ident[:, :])
                last.then_inc(p_ht, 1)

            def o_rows(n):
                k, i = divmod(n, TW)
                if i == 0:
                    pe.wait_ge(a_z, k + 1)
                if n >= 3:
                    pe.wait_ge(v_or, n - 2)
                pe.matmul(o_bank[n % 3][:, :], z_f[k % Z_RING][:, P * i:P * (i + 1)], w2_s, start=True, stop=True).then_inc(p_o, 1)

            pe.wait_ge(a_y, NT // 2 - 1)
            pe.wait_ge(v_y, NT // 2 - 1)
            pe.wait_ge(v_r, NT - IT)
            unit_split = {(ic, b): split[slot] for ic, b, slot, _ in loads[:UNITS]}
            outputs = output_plan(0)
            for at, (conv, k, ic, b, load) in enumerate(units):
                if load is not None:
                    pe.wait_ge(a_unit, load + 1)
                    pe.wait_ge(v_unit, load + 1)
                    unit_split[ic, b] = split[loads[load][2]]
                n = NC * conv + k
                if n == 0:
                    if b == Y_LAST[0]:
                        x1_transpose(NT - 2)
                        x1_transpose(NT - 1)
                    if b == Y_LAST[1]:
                        y_rows(NT // 2 - 1)
                    if b == NB - 1:
                        pe.wait_ge(a_y, NT // 2)
                        pe.wait_ge(v_y, NT // 2)
                if b == 0 and 2 <= n <= NC + 1:
                    pe.wait_ge(a_h, n - 1)
                if b == 0 and n > NC + 1:
                    pe.wait_ge(a_z, n - NC - 1)
                if conv == 1 and k == 0 and b == 0:
                    for g in range(H_BANKS):
                        h_transpose(g)
                if conv == 1 and k == 0 and b % 2 == 0:
                    pe.wait_ge(a_ht, b // 2 + 1)
                    pe.wait_ge(v_ht, b // 2 + 1)
                dst = acc_bank[n % 2][:, :].rearrange("p (i c) -> p i c", i=2)
                rhs = [unit_split[ic, b][:, part, :].rearrange("p (i j c) -> p i j c", i=2, j=IT) for part in range(2)]
                lhs = (y_hl, h_hl)[conv]
                for jj in range(IT):
                    wh, wl = lhs[:, 0, IT * b + jj, :], lhs[:, 1, IT * b + jj, :]
                    rh, rl = rhs[0][:, :, jj, :], rhs[1][:, :, jj, :]
                    pe.matmul(dst, wh, rh, start=(b == 0 and jj == 0), stop=False)
                    pe.matmul(dst, wh, rl, start=False, stop=False)
                    last = pe.matmul(dst, wl, rh, start=False, stop=(b == NB - 1 and jj == IT - 1))
                last.then_inc(p_unit, 1)
                if conv == 1 and k == 0 and b % 2 == 0 and b // 2 + H_BANKS < NC:
                    h_transpose(b // 2 + H_BANKS)
                for tile in outputs[at]:
                    if tile == 0:
                        pe.wait_ge(d_late, 32)
                        pe.wait_ge(v_r, NT)
                    o_rows(tile)
            for tile in outputs[-1]:
                o_rows(tile)

        @block.scalar
        def _(act):
            act.wait_ge(p_pre, 7)
            act.activation(col["c0"], bank[6][:, 0:1], ACT.Copy).then_inc(a_bias, 1)
            act.activation(c_row, bank[3][:, :], ACT.Copy).then_inc(a_bias, 1)
            act.wait_ge(v_sc, 1)
            act.wait_ge(p_pre, 7 + KD)
            for k in WVT_BLOCKS:
                act.activation(wvT[:, 0, k, :], wvt_bank[k][:, :], ACT.Identity, scale=col["s_wv"]).then_inc(a_pre, 1)
            for k in M_BLOCKS:
                act.activation(m_hl[:, 0, k, :], m_bank[k][:, :], ACT.Identity, scale=col["s_m"]).then_inc(a_pre, 1)

            def xt_hi(t):
                act.wait_ge(p_xt, t + 1)
                act.activation(xt_tiles[0][:, :, P * t:P * (t + 1)], xt_bank[t % 2][:, :].rearrange("p (k n) -> p k n", k=KD),
                               ACT.Identity, scale=col["s_x"]).then_inc(a_xt, 1)

            def g_hi(n):
                g, kk = divmod(n, KD)
                act.wait_ge(p_g, n + 1)
                if n >= 2:
                    act.wait_ge(v_g, n - 1)
                act.activation(g_row[n % 2], s_bank[n % 2][:, :], ACT.Identity, bias=gb_c[:, kk:kk + 1],
                               scale=col["k_gs"]).then_inc(a_gf, 1)
                if g >= 2 and kk == 0:
                    act.wait_ge(d_gout[g % 2], 32 * (g // 2))
                if n == 0:
                    act.wait_ge(p_pre, 11)
                act.wait_ge(a_gf, n + 1)
                act.activation(g_out[g % 2][:, 0, kk, :], g_row[n % 2], ACT.Copy).then_inc(a_g, 1)

            act.wait_ge(v_sx, 1)
            xt_hi(0)
            xt_hi(1)
            act.wait_ge(v_scales, 1)
            for t in range(NT):
                if 0 < t < NT - 1:
                    xt_hi(t + 1)
                if t % XG == 0 and t > 0:
                    g_hi(KD * (t // XG) - 1)
                act.wait_ge(v_vf, t + 1)
                act.wait_ge(v_c, t + 1)
                act.activation(v_hl[:, t, 0, :], v_row[t % 2], ACT.Identity, scale=col["s_v"]).then_inc(a_v, 1)
                if t % XG == XG - 1:
                    for kk in range(KD - 1):
                        g_hi(KD * (t // XG) + kk)
            g_hi(NT // XG * KD - 1)

            def x1_hi(t):
                act.wait_ge(p_x1t, t + 1)
                if t >= 2:
                    act.wait_ge(p_y, t // 2)
                act.activation(x1T[t % 2][:, 0, :], bank[t % 2][:, :], ACT.Copy, scale=X1_UP).then_inc(a_x1t, 1)

            def y_hi(n):
                act.wait_ge(p_y, n + 1)
                act.activation(y_hl[:, 0, 2 * n:2 * n + 2, :], a_bank[:, 0:2 * F].rearrange("p (t f) -> p t f", f=F),
                               ACT.Copy, scale=Y_DOWN).then_inc(a_y, 1)

            def h_out(n):
                act.wait_ge(v_hmax, n + 1)
                act.activation(hT[:, CW * n:CW * (n + 1)], acc_bank[n % 2][:, :], ACT.Relu, bias=b1_c[:, :],
                               scale=col["inv_h"]).then_inc(a_h, 1)

            def h_hi(g):
                act.wait_ge(p_ht, g + 1)
                act.activation(h_hl[:, 0, TW * g:TW * (g + 1), :], ht_bank[g % H_BANKS][:, :].rearrange("p (t f) -> p t f", f=F),
                               ACT.Copy).then_inc(a_ht, 1)

            def o_normalise(n):
                act.wait_ge(g_orstd, n + 1)
                i = n % O_RING
                o = o_row[i]
                act.activation(o, o, ACT.Identity, bias=shift[:, i:i + 1], scale=rstd[:, i:i + 1]).then_inc(a_o, 1)

            def load_residual(n):
                act.dma_start(x1_res[n % O_RING], x1_dram[output_rows(n), :]).then_inc(d_res[n % O_RING], 16)

            def store_output(n):
                act.wait_ge(a_o, n + 1)
                act.dma_start(out[output_rows(n), :], o_row[n % O_RING]).then_inc(d_out[n % O_RING], 16)
                if n + O_RING < NT:
                    load_residual(n + O_RING)

            def z_out(n):
                act.wait_ge(p_unit, NB * (NC + n + 1))
                if n >= Z_RING:
                    act.wait_ge(p_o, TW * (n - Z_RING + 1))
                act.activation(z_f[n % Z_RING], acc_bank[n % 2][:, :], ACT.Copy, scale=col["inv_z"]).then_inc(a_z, 1)

            def unit_hi(load):
                _, _, slot, after = loads[load]
                if load == 0:
                    act.wait_ge(v_sa, 1)
                act.wait_ge(d_raw[load % RAW_RING], 16 * (load // RAW_RING + 1))
                if PLAIN_SLOTS <= load < PLAIN_SLOTS + RING // 2:
                    last = NS - RING + 2 * (load - PLAIN_SLOTS) + 2
                    act.wait_ge(v_p, last)
                    act.wait_ge(g_den, last)
                elif load == PLAIN_SLOTS + RING // 2:
                    act.wait_ge(p_pv, NS)
                elif load == SLOTS - 1:
                    act.wait_ge(p_x1t, NT)
                    act.wait_ge(d_x1, 16 * NI)
                elif after:
                    act.wait_ge(p_unit, after)
                act.activation(split[slot][:, 0, :], raw[load % RAW_RING], ACT.Copy, scale=col["s_a"]).then_inc(a_unit, 1)

            for s in range(NS + LAG):
                if s < NS:
                    act.wait_ge(p_at, s + 1)
                    if s >= STAGE:
                        act.wait_ge(d_at[s % STAGE], 16 * (s // STAGE))
                        act.wait_ge(v_abs, s - STAGE + 1)
                    elif s == 0:
                        act.wait_ge(v_g, NT // XG * KD)
                        act.wait_ge(v_c, NT)
                    act.activation(stage[:, s % STAGE, :], a_bank[:, :], ACT.Copy).then_inc(a_at, 1)
                y = s - Y_FIRST
                if 0 < y < NT // 2:
                    y_hi(y - 1)
                e = s - EXP_LAG
                if 0 <= e < NS:
                    act.wait_ge(v_sub, e + 1)
                    p = ring[:, e % RING, :]
                    act.activation(p, p, ACT.Exp, scale=2.0).then_inc(a_exp, 1)
                    if e >= 2:
                        act.wait_ge(p_pv, e - 1)
                    act.wait_ge(a_exp, e + 1)
                    act.activation(pT[:, e % 2, 0, :], p, ACT.Copy, scale=P_UP).then_inc(a_p, 1)
                j, b = divmod(s, NB)
                if b == 0 and 1 <= j <= NI:
                    act.wait_ge(p_mr, j)
                    if j >= 2:
                        act.wait_ge(v_sub, NB * (j - 1))
                    act.activation(max_row[:, :], misc[:, 0:IW], ACT.Copy).then_inc(a_mr, 1)
                if s == NS:
                    act.wait_ge(d_w1, 16)
                    act.activation(w1_hl[:, 0, :, :].rearrange("p k f -> p (k f)"), w1_raw, ACT.Identity,
                                   scale=col["s_w1"]).then_inc(a_w1, 1)
                if 0 <= y < NT // 2 - 1:
                    x1_hi(2 * y)
                    x1_hi(2 * y + 1)
                if s >= NS + LAG - EARLY:
                    unit_hi(s - (NS + LAG - EARLY))

            normed, stored = output_plan(NORM_DELAY), output_plan(STORE_DELAY)
            for n, (conv, k, ic, b, _) in enumerate(units):
                for load in split_at[n]:
                    unit_hi(load)
                if conv == k == 0 and b == Y_LAST[0]:
                    x1_hi(NT - 2)
                    x1_hi(NT - 1)
                if conv == k == 0 and b == Y_LAST[1]:
                    y_hi(NT // 2 - 1)
                if conv == 1 and k == 0 and b == 0:
                    h_out(NC - 1)
                    for g in range(H_BANKS - 1):
                        h_hi(g)
                if conv == 1 and k == 0 and b % 2 == 0 and b // 2 + H_BANKS - 1 < NC:
                    h_hi(b // 2 + H_BANKS - 1)
                if b == OUT_AT and k >= 1:
                    (h_out, z_out)[conv](k - 1)
                if conv == 1 and k == 0 and b == NB // 2:
                    act.wait_ge(d_x1, 16 * NI)
                    act.wait_ge(p_y, NT // 2)
                    for tile in range(O_RING):
                        load_residual(tile)
                for tile in normed[n]:
                    o_normalise(tile)
                for tile in stored[n]:
                    store_output(tile)
            z_out(NC - 1)
            for tile in stored[-1]:
                if tile in normed[-1]:
                    o_normalise(tile)
                store_output(tile)
            for i in range(O_RING):
                act.wait_ge(d_out[i], 16 * (NT // O_RING))

        @block.vector
        def _(dve):
            chained = [0]

            def link(ins):
                chained[0] += 1
                ins.then_inc(v_chain, 1)
                dve.wait_ge(v_chain, chained[0])

            def abs_max(dst, src):
                return dve.tensor_reduce(dst, src, AX, ALU.max, apply_absolute_value=True)

            def power(dst, src):
                link(dve.tensor_scalar(dst, src, TINY, None, ALU.max))
                link(dve.tensor_scalar(dst.bitcast(U32), dst.bitcast(U32), EXP_BITS, None, ALU.bitwise_and))

            def scale_of(dst, power_of):
                link(dve.reciprocal(dst, power_of))
                link(dve.tensor_scalar(dst, dst, TOP, None, ALU.mult))

            def minus_hi(dst, src, scale, hi):
                return dve.scalar_tensor_tensor(dst, src, scale, hi, ALU.mult, ALU.subtract)

            def group_max(i):
                dve.wait_ge(d_x[i], 16)
                link(abs_max(x_max[:, i:i + 1], flat(xv[:, XG * i:XG * (i + 1), :])))

            dve.wait_ge(d_small, 16 * 5)
            abs_max(col["mx_bv"], bv_row).then_inc(v_st, 1)
            abs_max(col["st_w1"], w1_stat).then_inc(v_st, 1)
            dve.wait_ge(d_wv, 16)
            abs_max(col["st_wv"], flat(wv_raw)).then_inc(v_st, 1)
            for i in range(3):
                group_max(i)
            for k in range(KD):
                dve.wait_ge(p_pre, 1 + k)
                link(abs_max(col[f"m{k}"], m_bank[k][:, :]))
            dve.tensor_reduce(col["st_m"], cols("m0", "m3"), AX, ALU.max).then_inc(v_st, 1)
            group_max(3)
            group_max(4)
            dve.wait_ge(p_pre, 7)
            dve.tensor_scalar(gb_c[:, :], bank[2][:, 0:KD], LOGIT, None, ALU.mult).then_inc(v_pre, 1)
            dve.wait_ge(v_pre, 1)
            abs_max(col["st_gb"], gb_c[:, :]).then_inc(v_st, 1)
            group_max(5)
            dve.wait_ge(g_ar, 1)
            power(cols("e_m", "e_w1"), cols("mx_m", "mx_w1"))
            link(dve.reciprocal(cols("s_m", "s_w1"), cols("e_m", "e_w1")))
            dve.tensor_scalar(cols("s_m", "s_w1"), cols("s_m", "s_w1"), TOP, None, ALU.mult).then_inc(v_sc, 1)
            dve.wait_ge(v_sc, 1)
            group_max(6)
            group_max(7)
            dve.tensor_reduce(col["st_x"], x_max[:, :], AX, ALU.max).then_inc(v_st, 1)

            def wvt_lo(i):
                dve.wait_ge(a_pre, 1 + i)
                k = WVT_BLOCKS[i]
                minus_hi(wvT[:, 1, k, :], wvt_bank[k][:, :], col["s_wv"], wvT[:, 0, k, :]).then_inc(v_pre, 1)

            def m_lo(i):
                dve.wait_ge(a_pre, 1 + KD + i)
                k = M_BLOCKS[i]
                minus_hi(m_hl[:, 1, k, :], m_bank[k][:, :], col["s_m"], m_hl[:, 0, k, :]).then_inc(v_pre, 1)

            wvt_lo(0)
            wvt_lo(1)
            dve.wait_ge(g_ar, 2)
            power(col["e_x"], col["mx_x"])
            link(dve.reciprocal(col["s_x"], col["e_x"]))
            dve.tensor_scalar(col["s_x"], col["s_x"], TOP, None, ALU.mult).then_inc(v_sx, 1)
            dve.wait_ge(v_sx, 1)
            wvt_lo(2)

            def xt_lo(t):
                dve.wait_ge(a_xt, t + 1)
                minus_hi(xt_tiles[1][:, :, P * t:P * (t + 1)], xt_bank[t % 2][:, :].rearrange("p (k n) -> p k n", k=KD),
                         col["s_x"], xt_tiles[0][:, :, P * t:P * (t + 1)]).then_inc(v_xt, 1)

            xt_lo(0)
            wvt_lo(3)
            xt_lo(1)
            link(dve.tensor_scalar(col["k_g"], col["e_x"], col["e_m"], LOGIT / TOP ** 2, ALU.mult, ALU.mult))
            link(dve.tensor_scalar(col["k_v"], col["e_x"], col["e_wv"], 1 / TOP ** 2, ALU.mult, ALU.mult))
            link(dve.tensor_scalar(col["bound"], col["k_g"], 4.0 * D * TOP ** 2, col["mx_gb"], ALU.mult, ALU.add))
            power(col["e_g"], col["bound"])
            scale_of(col["s_g"], col["e_g"])
            link(dve.tensor_tensor(col["k_gs"], col["k_g"], col["s_g"], ALU.mult))
            link(dve.tensor_scalar(gb_c[:, :], gb_c[:, :], col["s_g"], None, ALU.mult))
            link(dve.tensor_scalar(col["k_l"], col["e_x"], col["e_g"], 1 / TOP ** 2, ALU.mult, ALU.mult))
            link(dve.tensor_scalar(col["bound"], col["k_v"], 4.0 * D * TOP ** 2, col["mx_bv"], ALU.mult, ALU.add))
            power(col["e_v"], col["bound"])
            scale_of(col["s_v"], col["e_v"])
            dve.tensor_scalar(col["k_u"], col["e_v"], 1 / (TOP * P_UP), None, ALU.mult).then_inc(v_scales, 1)
            dve.wait_ge(v_scales, 1)

            def g_lo(n):
                dve.wait_ge(a_g, n + 1)
                hi, lo = (g_out[n // KD % 2][:, part, n % KD, :] for part in range(2))
                dve.tensor_tensor(lo, g_row[n % 2], hi, ALU.subtract).then_inc(v_g, 1)

            def query_bias(t):
                dve.tensor_tensor_reduce(unused, xv[:, t, :], c_row, 1.0, 0.0, ALU.mult, ALU.add, col["t0"]).then_inc(v_c, 1)
                dve.wait_ge(v_c, t + 1)
                link(dve.tensor_scalar(c_all[:, t:t + 1], col["t0"], col["c0"], LOGIT, ALU.add, ALU.mult))

            m_lo(0)
            m_lo(1)
            dve.wait_ge(a_bias, 2)
            query_bias(0)
            for t in range(NT):
                if 0 < t < NT - 1:
                    xt_lo(t + 1)
                if t == 1:
                    m_lo(2)
                    m_lo(3)
                if t % XG == 0 and t > 0:
                    g_lo(KD * (t // XG) - 1)
                dve.wait_ge(p_v, t + 1)
                if t >= 2:
                    dve.wait_ge(a_v, t - 1)
                dve.scalar_tensor_tensor(v_row[t % 2], v_bank[t % U_BANKS][:, :], col["k_v"], bv_row,
                                         ALU.mult, ALU.add).then_inc(v_vf, 1)
                if t + 1 < NT:
                    query_bias(t + 1)
                dve.wait_ge(a_v, t + 1)
                dve.wait_ge(v_vf, t + 1)
                minus_hi(v_hl[:, t, 1, :], v_row[t % 2], col["s_v"], v_hl[:, t, 0, :]).then_inc(v_v, 1)
                if t % XG == XG - 1:
                    for kk in range(KD - 1):
                        g_lo(KD * (t // XG) + kk)
            g_lo(NT // XG * KD - 1)

            def halves(ap):
                return ap.rearrange("p (j i) -> p j i", j=IT)

            def subtract_max(e):
                if e % NB == 0:
                    dve.wait_ge(a_mr, e // NB + 1)
                    dve.wait_ge(v_run, e + NB)
                p = ring[:, e % RING, :]
                dve.tensor_tensor(halves(p), halves(p), max_row[:, :].unsqueeze(1).broadcast_to([P, IT, IW]),
                                  ALU.subtract).then_inc(v_sub, 1)

            def add_adj(s):
                dve.wait_ge(p_qk, s + 1)
                dve.wait_ge(a_at, s + 1)
                if s >= RING:
                    dve.wait_ge(a_p, s - RING + 1)
                    dve.wait_ge(v_p, s - RING + 1)
                    dve.wait_ge(g_den, s - RING + 1)
                elif s == 0:
                    for i in range(2):
                        dve.wait_ge(d_gout[i], 32 * (NT // XG // 2))
                dve.scalar_tensor_tensor(ring[:, s % RING, :], s_bank[s % 2][:, :], col["k_l"], stage[:, s % STAGE, :],
                                         ALU.mult, ALU.add).then_inc(v_add, 1)

            def running_max(s):
                dve.wait_ge(v_add, s + 1)
                b = s % NB
                if b >= 2:
                    dve.wait_ge(v_run, s)
                if b == 0:
                    return
                before = ring[:, (s - 1) % RING, :] if b == 1 else run_max[:, :]
                dve.tensor_tensor(run_max[:, :], before, ring[:, s % RING, :], ALU.max).then_inc(v_run, 1 + (b == 1))

            def fold_max(i):
                dve.wait_ge(v_run, NB * (i + 1))
                if i >= 1:
                    dve.wait_ge(p_mr, i)
                dve.tensor_tensor(fold[:, :], run_max[:, 0:IW], run_max[:, IW:2 * IW], ALU.max).then_inc(v_fold, 1)

            def max_diagonals(i):
                dve.wait_ge(p_mt, i + 1)
                link(dve.tensor_reduce(q_max[:, :], misc[:, 0:IW].rearrange("p (t n) -> p t n", t=IT), AX, ALU.max))
                c = c_all[:, IT * i:IT * (i + 1)]
                link(dve.tensor_tensor(q_max[:, :], q_max[:, :], c, ALU.add))
                link(dve.tensor_tensor(q_max[:, :], q_max[:, :], c, ALU.subtract))
                for t in range(IT):
                    last = dve.tensor_scalar(fold[:, P * t:P * (t + 1)], ident[:, :], q_max[:, t:t + 1], None, ALU.mult)
                    if t < IT - 1:
                        link(last)
                last.then_inc(v_diag, 1)

            def p_lo(e):
                dve.wait_ge(a_p, e + 1)
                minus_hi(pT[:, e % 2, 1, :], ring[:, e % RING, :], P_UP, pT[:, e % 2, 0, :]).then_inc(v_p, 1)

            def adj_maximum(s):
                i, b = divmod(s, NB)
                abs_max(adj_max[:, b:b + 1], stage[:, s % STAGE, :]).then_inc(v_abs, 1)
                if b == NB - 1:
                    dve.wait_ge(v_abs, s + 1)
                    link(dve.tensor_reduce(adj_all[:, i:i + 1], adj_max[:, :], AX, ALU.max))

            def attention_rows(i, t):
                r = xr[:, t, :]
                if t == 0:
                    dve.wait_ge(p_pv, NB * (i + 1))
                    dve.wait_ge(p_den, i + 1)
                    dve.wait_ge(d_xr, 16 * (i + 1))
                link(dve.reciprocal(col["t0"], misc[:, t:t + 1]))
                link(dve.tensor_scalar(col["t1"], col["t0"], col["k_u"], None, ALU.mult))
                dve.scalar_tensor_tensor(r, u_bank[IT * (i % 2) + t][:, :], col["t1"], r, ALU.mult, ALU.add).then_inc(v_r, 1)
                dve.wait_ge(v_r, IT * i + t + 1)
                link(dve.bn_stats(bn[:, :], r))
                link(dve.bn_aggr(mv[:, t, :], bn[:, :]))
                ins = dve.tensor_scalar(veps[:, t:t + 1], mv[:, t, 1:2], EPS, None, ALU.add)
                if t == IT - 1:
                    ins.then_inc(v_var, 1)

            def normalise(i):
                dve.wait_ge(g_rstd, i + 1)
                for t in range(IT):
                    ins = dve.tensor_scalar(xr[:, t, :], xr[:, t, :], mv[:, t, 0:1], rstd[:, t:t + 1], ALU.subtract, ALU.mult)
                ins.then_inc(v_x1, 1)

            def x1_lo(t):
                dve.wait_ge(a_x1t, t + 1)
                minus_hi(x1T[t % 2][:, 1, :], bank[t % 2][:, :], X1_UP, x1T[t % 2][:, 0, :]).then_inc(v_x1t, 1)

            def y_lo(n):
                dve.wait_ge(a_y, n + 1)
                minus_hi(y_hl[:, 1, 2 * n:2 * n + 2, :].rearrange("p t f -> p (t f)"), a_bank[:, 0:2 * F], Y_DOWN,
                         y_hl[:, 0, 2 * n:2 * n + 2, :].rearrange("p t f -> p (t f)")).then_inc(v_y, 1)

            def unit_lo(load):
                slot = loads[load][2]
                dve.wait_ge(a_unit, load + 1)
                minus_hi(split[slot][:, 1, :], raw[load % RAW_RING], col["s_a"], split[slot][:, 0, :]).then_inc(v_unit, 1)

            for s in range(NS + LAG + 4):
                j, b = divmod(s, NB)
                e = s - EXP_LAG
                if 0 <= e < NS:
                    subtract_max(e)
                if s < NS:
                    add_adj(s)
                    if b == 0 and j >= 1:
                        max_diagonals(j - 1)
                    running_max(s)
                    if b == NB - 1:
                        fold_max(j)
                elif s == NS:
                    max_diagonals(j - 1)
                y = s - Y_FIRST
                if 0 < y < NT // 2:
                    y_lo(y - 1)
                if NS + LAG - EARLY < s <= NS + LAG:
                    unit_lo(s - 1 - (NS + LAG - EARLY))
                if 0 <= y < NT // 2 - 1:
                    x1_lo(2 * y)
                    x1_lo(2 * y + 1)
                if 0 <= e < NS:
                    p_lo(e)
                if s < NS:
                    adj_maximum(s)
                if 2 <= b < 2 + IT and j >= 2:
                    attention_rows(j - 2, b - 2)
                if b == 2 + IT and j >= 2:
                    normalise(j - 2)
                if s == NS:
                    dve.tensor_reduce(col["st_a"], adj_all[:, :], AX, ALU.max).then_inc(v_st, 1)
                    dve.wait_ge(a_w1, 1)
                    minus_hi(w1_hl[:, 1, :, :].rearrange("p k f -> p (k f)"), w1_raw, col["s_w1"],
                             w1_hl[:, 0, :, :].rearrange("p k f -> p (k f)")).then_inc(v_w1, 1)
                if s == NS + 4:
                    dve.wait_ge(g_ar, 3)
                    power(col["e_a"], col["mx_a"])
                    scale_of(col["s_a"], col["e_a"])
                    dve.tensor_scalar(col["inv_h"], col["e_a"], col["e_w1"], 1 / (TOP * TOP * X1_UP * Y_DOWN),
                                      ALU.mult, ALU.mult).then_inc(v_sa, 1)

            def o_stats(n):
                i = n % O_RING
                o = o_row[i]
                dve.wait_ge(p_o, n + 1)
                dve.wait_ge(g_res, n + 1)
                if n >= O_RING:
                    dve.wait_ge(d_out[n % O_RING], 16 * (n // O_RING))
                dve.tensor_tensor(o, o_bank[n % 3][:, :], x1_res[n % O_RING], ALU.add).then_inc(v_or, 1)
                dve.wait_ge(v_or, n + 1)
                link(dve.bn_stats(bn[:, :], o))
                if n >= O_RING:
                    dve.wait_ge(g_orstd, n - O_RING + 1)
                link(dve.bn_aggr(mv[:, i, :], bn[:, :]))
                dve.tensor_scalar(veps[:, i:i + 1], mv[:, i, 1:2], EPS, None, ALU.add).then_inc(v_ovar, 1)

            def h_maximum(n):
                dve.wait_ge(p_unit, NB * (n + 1))
                dve.tensor_reduce(h_max[:, n:n + 1], acc_bank[n % 2][:, :], AX, ALU.max).then_inc(v_hmax, 1)

            def h_scaled(g):
                dve.wait_ge(a_h, g + 1)
                h = hT[:, CW * g:CW * (g + 1)]
                dve.tensor_scalar(h, h, col["s_h"], None, ALU.mult).then_inc(v_h, 1)

            def h_lo(g):
                dve.wait_ge(a_ht, g + 1)
                minus_hi(h_hl[:, 1, TW * g:TW * (g + 1), :].rearrange("p t f -> p (t f)"), ht_bank[g % H_BANKS][:, :], 1.0,
                         h_hl[:, 0, TW * g:TW * (g + 1), :].rearrange("p t f -> p (t f)")).then_inc(v_ht, 1)

            measured = output_plan(STATS_DELAY)
            for n, (conv, k, ic, b, _) in enumerate(units):
                for load in split_at[n]:
                    unit_lo(load)
                if conv == k == 0 and b == Y_LAST[0]:
                    x1_lo(NT - 2)
                    x1_lo(NT - 1)
                if conv == k == 0 and b == Y_LAST[1]:
                    y_lo(NT // 2 - 1)
                if conv == 0 and k >= 1 and b == OUT_AT:
                    h_maximum(k - 1)
                if conv == 1 and k == 0 and b == 0:
                    h_maximum(NC - 1)
                    dve.wait_ge(v_hmax, NC)
                    link(dve.tensor_reduce(col["t0"], h_max[:, :], AX, ALU.max))
                    link(dve.tensor_scalar(col["t0"], col["t0"], col["inv_h"], b1_c[:, :], ALU.mult, ALU.add))
                    power(col["e_h"], col["t0"])
                    scale_of(col["s_h"], col["e_h"])
                    for g in range(H_BANKS):
                        h_scaled(g)
                    for g in range(H_BANKS - 1):
                        h_lo(g)
                    link(dve.tensor_scalar(col["inv_z"], col["e_h"], col["e_a"], 1 / TOP ** 2, ALU.mult, ALU.mult))
                if conv == 1 and k == 0 and b % 2 == 0:
                    if b // 2 + H_BANKS < NC:
                        h_scaled(b // 2 + H_BANKS)
                    if b // 2 + H_BANKS - 1 < NC:
                        h_lo(b // 2 + H_BANKS - 1)
                for tile in measured[n]:
                    o_stats(tile)
            for tile in measured[-1]:
                o_stats(tile)

        @block.gpsimd
        def _(pool):
            pool.memset(ident[:, :], 0.0).then_inc(g_id, 1)
            pool.memset(ones[:, :], 1.0)
            pool.memset(col["minus_half"], -0.5)
            pool.memset(col["minus_one"], -1.0)
            pool.wait_ge(g_id, 1)
            pool.affine_select(out=ident[:, :], in_=ident[:, :], compare_op=ALU.not_equal, fill=1.0, base=0,
                               pattern=[[-1, P]], channel_multiplier=1).then_inc(g_id, 1)
            pool.wait_ge(v_st, 5)
            pool.partition_all_reduce(cols("mx_m", "mx_gb"), cols("st_m", "st_gb"), P, ALL_MAX).then_inc(g_ar, 1)
            pool.wait_ge(v_st, 6)
            pool.partition_all_reduce(col["mx_x"], col["st_x"], P, ALL_MAX).then_inc(g_ar, 1)
            for s in range(NS + LAG + 4):
                e = s - EXP_LAG
                if 0 <= e < NS:
                    i, b = divmod(e, NB)
                    pool.wait_ge(a_exp, e + 1)
                    if b == 0 and i >= 1:
                        pool.wait_ge(p_den, i)
                    if b == 0:
                        pool.tensor_copy(den[:, :], ring[:, e % RING, :]).then_inc(g_den, 1)
                    else:
                        pool.wait_ge(g_den, e)
                        pool.tensor_tensor(den[:, :], den[:, :], ring[:, e % RING, :], ALU.add).then_inc(g_den, 1)
                if s % NB == 1 + IT and s // NB >= 2:
                    i = s // NB - 2
                    pool.wait_ge(v_var, i + 1)
                    for t in range(IT):
                        last = pool.tensor_tensor(rstd[:, t:t + 1], veps[:, t:t + 1], col["minus_half"], ALU.pow)
                    last.then_inc(g_rstd, 1)
                if s == NS + 1:
                    pool.wait_ge(v_st, 7)
                    pool.partition_all_reduce(col["mx_a"], col["st_a"], P, ALL_MAX).then_inc(g_ar, 1)

            def residual(n):
                pool.wait_ge(d_res[n % O_RING], 16 * (n // O_RING + 1))
                pool.tensor_tensor(x1_res[n % O_RING], x1_res[n % O_RING], b2_row, ALU.add).then_inc(g_res, 1)

            pool.wait_ge(d_late, 32)
            for n in range(3):
                residual(n)
            for n in range(NT):
                i = n % O_RING
                pool.wait_ge(v_ovar, n + 1)
                if n >= O_RING:
                    pool.wait_ge(a_o, n - O_RING + 1)
                pool.tensor_tensor(minus_mean[:, i:i + 1], mv[:, i, 0:1], col["minus_one"], ALU.mult).then_inc(g_norm, 1)
                pool.tensor_tensor(rstd[:, i:i + 1], veps[:, i:i + 1], col["minus_half"], ALU.pow).then_inc(g_norm, 1)
                pool.wait_ge(g_norm, 2 * (n + 1))
                pool.tensor_tensor(shift[:, i:i + 1], minus_mean[:, i:i + 1], rstd[:, i:i + 1], ALU.mult).then_inc(g_orstd, 1)
                if n + 3 < NT:
                    residual(n + 3)


_INPUTS = ["x", "adj", "L0_gnn_Wq", "L0_gnn_bq", "L0_gnn_Wk", "L0_gnn_bk", "L0_gnn_Wv", "L0_gnn_bv",
           "L1_gnn_W1", "L1_gnn_b1", "L1_gnn_W2", "L1_gnn_b2"]


def kernel(**inputs):
    import numpy as np
    import concourse.bacc as bacc
    from concourse.bass_utils import run_bass_kernel_spmd

    nc = bacc.Bacc("TRN2", target_bir_lowering=False, num_devices=1)
    arrays = {f"in_{name}": np.ascontiguousarray(inputs[name]) for name in _INPUTS}
    args = [nc.dram_tensor(name, a.shape, mybir.dt.from_np(a.dtype), kind="ExternalInput").ap() for name, a in arrays.items()]
    out = nc.dram_tensor("out", (N, D), F32, kind="ExternalOutput").ap()
    x1_dram = nc.dram_tensor("x1_dram", (N, D), F32, kind="Internal").ap()
    g_dram = nc.dram_tensor("g_dram", (NI, P, 2 * KD * IW), F16, kind="Internal").ap()
    at_dram = nc.dram_tensor("at_dram", (NS, P, BANK), F32, kind="Internal").ap()
    gnn_program(nc, *args, out, x1_dram, g_dram, at_dram)
    return run_bass_kernel_spmd(nc, [arrays], core_ids=[0]).results[0]["out"]
```
